# Optimizing a Trainium2 kernel written in Bass

```python
import numpy as np
import jax
import jax.numpy as jnp

def _softmax(x, axis=-1):
    return jax.nn.softmax(x, axis=axis)

def _gelu(x):
    return jax.nn.gelu(x, approximate=True)

def _silu(x):
    return jax.nn.silu(x)

def _sigmoid(x):
    return jax.nn.sigmoid(x)

def _layernorm(x, axis=-1, eps=1e-05):
    m = jnp.mean(x, axis=axis, keepdims=True)
    v = jnp.var(x, axis=axis, keepdims=True)
    return (x - m) / jnp.sqrt(v + eps)

def _scatter_add(tgt, idx, src, axis=0):
    return tgt.at[idx].add(src)

def _segment_sum(src, seg, n):
    return jax.ops.segment_sum(src, seg, n)
kernel_name = 'mk_flamingo_gated_d2_seqx_r4_d6b766'

def setup_inputs(seed: int=0):
    np.random.seed(seed)
    _w = jnp.asarray

    def _rec_inputs():
        import jax
        import jax.numpy as jnp
        _rk = jax.random.key(seed)
        x = -1.394e-06 + 0.9999 * jax.random.normal(jax.random.fold_in(_rk, 1), (2, 1024, 256), jnp.float32)
        _lenS = 1024 - jax.random.randint(jax.random.fold_in(_rk, 7), (2,), 0, max(1, 1024 // 4) + 1, jnp.int32)
        _lenS2 = 77 - jax.random.randint(jax.random.fold_in(_rk, 8), (2,), 0, max(1, 77 // 4) + 1, jnp.int32)
        _ctx_1024P = jax.random.normal(jax.random.fold_in(_rk, 11), (2, 16, 256), jnp.float32)
        _ctx_1024c = jax.random.dirichlet(jax.random.fold_in(_rk, 511), 0.3 * jnp.ones((16,), jnp.float32), (2, 77))
        _ctx_1024t = jnp.einsum('bsk,bkd->bsd', _ctx_1024c, _ctx_1024P)
        _ctx_1024t = _ctx_1024t * jax.lax.rsqrt(jnp.mean(jnp.square(_ctx_1024t)) + 1e-12) * 0.953939
        ctx_1024 = -0.000392918 + 0.999932 * (_ctx_1024t + 0.3 * jax.random.normal(jax.random.fold_in(_rk, 611), (2, 77, 256), jnp.float32))
        _validS = jnp.arange(1024)[None, :] < _lenS[:, None]
        _validS2 = jnp.arange(77)[None, :] < _lenS2[:, None]
        _causal = jnp.tril(jnp.ones((1024, 1024), dtype=bool))
        mask_BxS2_bk0 = jnp.logical_not(jnp.broadcast_to(_validS2[:, :], (2, 77)))
        _g = jax.random.normal(jax.random.fold_in(_rk, 9001), (2, 2), jnp.float32)
        _g = jnp.sign(_g) * jnp.maximum(jnp.abs(_g), 1.0) + (_g == 0) * 1.0
        g_xattn = _g[0]
        g_ffn = _g[1]
        return (x, ctx_1024, mask_BxS2_bk0, g_xattn, g_ffn)
    x, ctx_1024, mask_BxS2_bk0, g_xattn, g_ffn = _rec_inputs()

    def _L0_xattn_setup():
        import jax, jax.numpy as jnp
        import numpy as np
        DIM = 256
        DIM_LATENT = 256
        DIM_HEAD = 64
        INNER = max(DIM, DIM_LATENT)
        HEADS = INNER // DIM_HEAD
        SCALE = DIM_HEAD ** (-0.5)
        LN_EPS = 1e-05
        RMS_EPS = 1e-08

        def layernorm(x, g, b):
            mu = jnp.mean(x, axis=-1, keepdims=True)
            var = jnp.mean(jnp.square(x - mu), axis=-1, keepdims=True)
            return (x - mu) * jax.lax.rsqrt(var + LN_EPS) * g + b

        def rmsnorm(x, gamma):
            n = jnp.linalg.norm(x, axis=-1, keepdims=True) * x.shape[-1] ** (-0.5)
            return x / jnp.maximum(n, RMS_EPS) * gamma
        key = jax.random.key(seed)
        ks = jax.random.split(key, 8)
        b, n, nl = (8, 512, 128)
        x = jax.random.normal(ks[0], (b, n, DIM), dtype=jnp.float32)
        latents = jax.random.normal(ks[1], (b, nl, DIM_LATENT), dtype=jnp.float32)
        mask = jax.random.randint(ks[2], (b, n), 0, 2).astype(bool)
        init = lambda k, shape, fan_in: jax.random.normal(k, shape, jnp.float32) * fan_in ** (-0.5)
        return {'x': x, 'latents': latents, 'mask': mask, 'ln_x_g': jnp.ones((DIM,), jnp.float32), 'ln_x_b': jnp.zeros((DIM,), jnp.float32), 'ln_l_g': jnp.ones((DIM_LATENT,), jnp.float32), 'ln_l_b': jnp.zeros((DIM_LATENT,), jnp.float32), 'q_gamma': jnp.ones((DIM_HEAD,), jnp.float32), 'k_gamma': jnp.ones((DIM_HEAD,), jnp.float32), 'W_q': init(ks[3], (DIM_LATENT, INNER), DIM_LATENT), 'W_kv': init(ks[4], (DIM, 2 * INNER), DIM), 'W_out': init(ks[5], (INNER, DIM_LATENT), INNER), 'b_out': jnp.zeros((DIM_LATENT,), jnp.float32)}
    _L0_xattn_all = _L0_xattn_setup()
    _L0_xattn_in = {k: v for k, v in _L0_xattn_all.items() if k in ('ln_x_g', 'ln_x_b', 'ln_l_g', 'ln_l_b', 'q_gamma', 'k_gamma', 'W_q', 'W_kv', 'W_out', 'b_out')}
    del _L0_xattn_all

    def _L0_ffn_setup():
        import jax, jax.numpy as jnp
        import numpy as np
        import math
        BETA = 0.9
        THRESHOLD = 1.0
        NUM_STEPS = 5
        ALPHA = 2.0

        @jax.custom_vjp
        def spike_fn(u):
            return (u > 0).astype(u.dtype)

        def _spike_fwd(u):
            return (spike_fn(u), u)

        def _spike_bwd(u, g):
            s = jnp.pi / 2.0 * ALPHA * u
            return (g * (ALPHA / 2.0) / (1.0 + s * s),)
        spike_fn.defvjp(_spike_fwd, _spike_bwd)
        key = jax.random.key(seed)
        k1, k2, k3 = jax.random.split(key, 3)
        n_embd = 256
        x = jax.random.normal(k1, (4, 512, n_embd), dtype=jnp.float32)
        W_fc = jax.random.normal(k2, (4 * n_embd, n_embd), dtype=jnp.float32) / math.sqrt(n_embd)
        W_proj = jax.random.normal(k3, (n_embd, 4 * n_embd), dtype=jnp.float32) / math.sqrt(4 * n_embd)
        return {'x': x, 'W_fc': W_fc, 'W_proj': W_proj}
    _L0_ffn_all = _L0_ffn_setup()
    _L0_ffn_in = {k: v for k, v in _L0_ffn_all.items() if k in ('W_fc', 'W_proj')}
    del _L0_ffn_all

    def _L1_xattn_setup():
        import jax, jax.numpy as jnp
        import numpy as np
        N_HEAD, MODEL_DIM, KEY_DIM, VALUE_DIM = (16, 256, 64, 64)
        B, S = (4, 512)
        EPS = 1e-05
        TEMP = float(np.sqrt(KEY_DIM))
        key = jax.random.key(seed)
        ks = jax.random.split(key, 12)
        d = {'query': jax.random.normal(ks[0], (B, S, MODEL_DIM), jnp.float32), 'key': jax.random.normal(ks[1], (B, S, MODEL_DIM), jnp.float32), 'value': jax.random.normal(ks[2], (B, S, MODEL_DIM), jnp.float32), 'Wq': jax.random.normal(ks[3], (MODEL_DIM, N_HEAD * KEY_DIM), jnp.float32) * np.sqrt(2.0 / (MODEL_DIM + KEY_DIM)), 'bq': jnp.zeros((N_HEAD * KEY_DIM,), jnp.float32), 'Wk': jax.random.normal(ks[4], (MODEL_DIM, N_HEAD * KEY_DIM), jnp.float32) * np.sqrt(2.0 / (MODEL_DIM + KEY_DIM)), 'bk': jnp.zeros((N_HEAD * KEY_DIM,), jnp.float32), 'Wv': jax.random.normal(ks[5], (MODEL_DIM, N_HEAD * VALUE_DIM), jnp.float32) * np.sqrt(2.0 / (MODEL_DIM + VALUE_DIM)), 'bv': jnp.zeros((N_HEAD * VALUE_DIM,), jnp.float32), 'Wo': jax.random.normal(ks[6], (N_HEAD * VALUE_DIM, MODEL_DIM), jnp.float32) * np.sqrt(2.0 / (N_HEAD * VALUE_DIM + MODEL_DIM)), 'bo': jnp.zeros((MODEL_DIM,), jnp.float32), 'ln_gamma': jnp.ones((MODEL_DIM,), jnp.float32), 'ln_beta': jnp.zeros((MODEL_DIM,), jnp.float32)}
        return d
    _L1_xattn_all = _L1_xattn_setup()
    _L1_xattn_in = {k: v for k, v in _L1_xattn_all.items() if k in ('Wq', 'bq', 'Wk', 'bk', 'Wv', 'bv', 'Wo', 'bo', 'ln_gamma', 'ln_beta')}
    del _L1_xattn_all

    def _L1_ffn_setup():
        import jax, jax.numpy as jnp
        import numpy as np
        B, S, D, F, E = (4, 512, 256, 1024, 8)
        LN_EPS = 1e-05
        key = jax.random.key(seed)
        ks = jax.random.split(key, 6)
        sc = 0.02
        return {'x': jax.random.normal(ks[0], (B, S, D), dtype=jnp.float32), 'Wr': jax.random.normal(ks[1], (D, E), dtype=jnp.float32) * sc, 'br': jnp.zeros((E,), jnp.float32), 'ln_g': jnp.ones((D,), jnp.float32), 'ln_b': jnp.zeros((D,), jnp.float32), 'W1': jax.random.normal(ks[2], (E, D, F), dtype=jnp.float32) * sc, 'b1': jnp.zeros((E, F), jnp.float32), 'W2': jax.random.normal(ks[3], (E, F, D), dtype=jnp.float32) * sc, 'b2': jnp.zeros((E, D), jnp.float32)}
    _L1_ffn_all = _L1_ffn_setup()
    _L1_ffn_in = {k: v for k, v in _L1_ffn_all.items() if k in ('Wr', 'br', 'ln_g', 'ln_b', 'W1', 'b1', 'W2', 'b2')}
    del _L1_ffn_all
    return {'x': x, 'ctx_1024': ctx_1024, 'mask_BxS2_bk0': mask_BxS2_bk0, 'g_xattn': g_xattn, 'g_ffn': g_ffn, 'L0_xattn_ln_x_g': _L0_xattn_in['ln_x_g'], 'L0_xattn_ln_x_b': _L0_xattn_in['ln_x_b'], 'L0_xattn_ln_l_g': _L0_xattn_in['ln_l_g'], 'L0_xattn_ln_l_b': _L0_xattn_in['ln_l_b'], 'L0_xattn_q_gamma': _L0_xattn_in['q_gamma'], 'L0_xattn_k_gamma': _L0_xattn_in['k_gamma'], 'L0_xattn_W_q': _L0_xattn_in['W_q'], 'L0_xattn_W_kv': _L0_xattn_in['W_kv'], 'L0_xattn_W_out': _L0_xattn_in['W_out'], 'L0_xattn_b_out': _L0_xattn_in['b_out'], 'L0_ffn_W_fc': _L0_ffn_in['W_fc'], 'L0_ffn_W_proj': _L0_ffn_in['W_proj'], 'L1_xattn_Wq': _L1_xattn_in['Wq'], 'L1_xattn_bq': _L1_xattn_in['bq'], 'L1_xattn_Wk': _L1_xattn_in['Wk'], 'L1_xattn_bk': _L1_xattn_in['bk'], 'L1_xattn_Wv': _L1_xattn_in['Wv'], 'L1_xattn_bv': _L1_xattn_in['bv'], 'L1_xattn_Wo': _L1_xattn_in['Wo'], 'L1_xattn_bo': _L1_xattn_in['bo'], 'L1_xattn_ln_gamma': _L1_xattn_in['ln_gamma'], 'L1_xattn_ln_beta': _L1_xattn_in['ln_beta'], 'L1_ffn_Wr': _L1_ffn_in['Wr'], 'L1_ffn_br': _L1_ffn_in['br'], 'L1_ffn_ln_g': _L1_ffn_in['ln_g'], 'L1_ffn_ln_b': _L1_ffn_in['ln_b'], 'L1_ffn_W1': _L1_ffn_in['W1'], 'L1_ffn_b1': _L1_ffn_in['b1'], 'L1_ffn_W2': _L1_ffn_in['W2'], 'L1_ffn_b2': _L1_ffn_in['b2']}

def reference(x, ctx_1024, mask_BxS2_bk0, g_xattn, g_ffn, L0_xattn_ln_x_g, L0_xattn_ln_x_b, L0_xattn_ln_l_g, L0_xattn_ln_l_b, L0_xattn_q_gamma, L0_xattn_k_gamma, L0_xattn_W_q, L0_xattn_W_kv, L0_xattn_W_out, L0_xattn_b_out, L0_ffn_W_fc, L0_ffn_W_proj, L1_xattn_Wq, L1_xattn_bq, L1_xattn_Wk, L1_xattn_bk, L1_xattn_Wv, L1_xattn_bv, L1_xattn_Wo, L1_xattn_bo, L1_xattn_ln_gamma, L1_xattn_ln_beta, L1_ffn_Wr, L1_ffn_br, L1_ffn_ln_g, L1_ffn_ln_b, L1_ffn_W1, L1_ffn_b1, L1_ffn_W2, L1_ffn_b2):
    import jax
    import jax.numpy as jnp

    def _L0_xattn_ref(x, latents, mask, ln_x_g, ln_x_b, ln_l_g, ln_l_b, q_gamma, k_gamma, W_q, W_kv, W_out, b_out):
        import jax, jax.numpy as jnp
        import numpy as np
        DIM = 256
        DIM_LATENT = 256
        DIM_HEAD = 64
        INNER = max(DIM, DIM_LATENT)
        HEADS = INNER // DIM_HEAD
        SCALE = DIM_HEAD ** (-0.5)
        LN_EPS = 1e-05
        RMS_EPS = 1e-08

        def layernorm(x, g, b):
            mu = jnp.mean(x, axis=-1, keepdims=True)
            var = jnp.mean(jnp.square(x - mu), axis=-1, keepdims=True)
            return (x - mu) * jax.lax.rsqrt(var + LN_EPS) * g + b

        def rmsnorm(x, gamma):
            n = jnp.linalg.norm(x, axis=-1, keepdims=True) * x.shape[-1] ** (-0.5)
            return x / jnp.maximum(n, RMS_EPS) * gamma
        b, n, _ = x.shape
        nl = latents.shape[1]
        xn = layernorm(x, ln_x_g, ln_x_b)
        ln = layernorm(latents, ln_l_g, ln_l_b)
        q = ln @ W_q
        kv = jnp.concatenate([xn @ W_kv, ln @ W_kv], axis=1)
        k, v = (kv[..., :INNER], kv[..., INNER:])
        to_heads = lambda t: t.reshape(t.shape[0], t.shape[1], HEADS, DIM_HEAD).transpose(0, 2, 1, 3)
        q, k, v = (to_heads(q), to_heads(k), to_heads(v))
        qn = rmsnorm(q, q_gamma) * SCALE
        kn = rmsnorm(k, k_gamma)
        sim = jnp.einsum('bhid,bhjd->bhij', qn, kn)
        full_mask = jnp.pad(mask, ((0, 0), (0, nl)), constant_values=True)
        neg = -jnp.finfo(sim.dtype).max
        sim = jnp.where(full_mask[:, None, None, :], sim, neg)
        attn = jax.nn.softmax(sim.astype(jnp.float32), axis=-1).astype(sim.dtype)
        out = jnp.einsum('bhij,bhjd->bhid', attn, v)
        out = out.transpose(0, 2, 1, 3).reshape(b, nl, INNER)
        return out @ W_out + b_out

    def _L0_ffn_ref(x, W_fc, W_proj):
        import jax, jax.numpy as jnp
        import numpy as np
        import math
        BETA = 0.9
        THRESHOLD = 1.0
        NUM_STEPS = 5
        ALPHA = 2.0

        @jax.custom_vjp
        def spike_fn(u):
            return (u > 0).astype(u.dtype)

        def _spike_fwd(u):
            return (spike_fn(u), u)

        def _spike_bwd(u, g):
            s = jnp.pi / 2.0 * ALPHA * u
            return (g * (ALPHA / 2.0) / (1.0 + s * s),)
        spike_fn.defvjp(_spike_fwd, _spike_bwd)
        h = jnp.square(jax.nn.relu(jnp.einsum('bsd,fd->bsf', x, W_fc)))
        y = jnp.einsum('bsf,df->bsd', h, W_proj)

        def step(mem, _):
            reset = jax.lax.stop_gradient(spike_fn(mem - THRESHOLD))
            mem_new = BETA * mem + y - reset * THRESHOLD
            spk = spike_fn(mem_new - THRESHOLD)
            return (mem_new, spk)
        mem0 = jnp.zeros_like(y)
        _, spks = jax.lax.scan(step, mem0, None, length=NUM_STEPS)
        return jnp.sum(spks, axis=0) / NUM_STEPS

    def _L1_xattn_ref(query, key, value, Wq, bq, Wk, bk, Wv, bv, Wo, bo, ln_gamma, ln_beta):
        import jax, jax.numpy as jnp
        import numpy as np
        N_HEAD, MODEL_DIM, KEY_DIM, VALUE_DIM = (16, 256, 64, 64)
        B, S = (4, 512)
        EPS = 1e-05
        TEMP = float(np.sqrt(KEY_DIM))
        b, sq, _ = query.shape
        residual = query
        q = (query @ Wq + bq).reshape(b, sq, N_HEAD, KEY_DIM)
        k = (key @ Wk + bk).reshape(b, key.shape[1], N_HEAD, KEY_DIM)
        v = (value @ Wv + bv).reshape(b, value.shape[1], N_HEAD, VALUE_DIM)
        scores = jnp.einsum('bqhd,bkhd->bhqk', q, k) / TEMP
        attn = jax.nn.softmax(scores, axis=-1)
        out = jnp.einsum('bhqk,bkhd->bqhd', attn, v).reshape(b, sq, N_HEAD * VALUE_DIM)
        out = out @ Wo + bo + residual
        mu = jnp.mean(out, axis=-1, keepdims=True)
        var = jnp.var(out, axis=-1, keepdims=True)
        return (out - mu) * jax.lax.rsqrt(var + EPS) * ln_gamma + ln_beta

    def _L1_ffn_ref(x, Wr, br, ln_g, ln_b, W1, b1, W2, b2):
        import jax, jax.numpy as jnp
        import numpy as np
        B, S, D, F, E = (4, 512, 256, 1024, 8)
        LN_EPS = 1e-05
        tokens_shape = x.shape[:-1]
        xt = x.reshape(-1, x.shape[-1])
        router_logits = xt @ Wr + br
        router_probs = jax.nn.softmax(router_logits, axis=-1)
        gates = jnp.max(router_probs, axis=-1, keepdims=True)
        idx = jnp.argmax(router_probs, axis=-1)
        onehot = jax.nn.one_hot(idx, E, dtype=xt.dtype)
        mu = jnp.mean(xt, axis=-1, keepdims=True)
        var = jnp.mean(jnp.square(xt - mu), axis=-1, keepdims=True)
        xn = (xt - mu) * jax.lax.rsqrt(var + LN_EPS) * ln_g + ln_b
        h = jnp.einsum('te,td,edf->tf', onehot, xn, W1) + b1[idx]
        h = jax.nn.relu(h)
        y = jnp.einsum('te,tf,efd->td', onehot, h, W2) + b2[idx]
        y = y * gates
        return y.reshape(tokens_shape + (y.shape[-1],))
    x = x + jnp.tanh(g_xattn[0]) * _L0_xattn_ref(ctx_1024, _layernorm(x, axis=-1), mask_BxS2_bk0, L0_xattn_ln_x_g, L0_xattn_ln_x_b, L0_xattn_ln_l_g, L0_xattn_ln_l_b, L0_xattn_q_gamma, L0_xattn_k_gamma, L0_xattn_W_q, L0_xattn_W_kv, L0_xattn_W_out, L0_xattn_b_out)
    x = x + jnp.tanh(g_ffn[0]) * _L0_ffn_ref(_layernorm(x, axis=-1), L0_ffn_W_fc, L0_ffn_W_proj)
    x = x + jnp.tanh(g_xattn[1]) * _L1_xattn_ref(_layernorm(x, axis=-1), ctx_1024, ctx_1024, L1_xattn_Wq, L1_xattn_bq, L1_xattn_Wk, L1_xattn_bk, L1_xattn_Wv, L1_xattn_bv, L1_xattn_Wo, L1_xattn_bo, L1_xattn_ln_gamma, L1_xattn_ln_beta)
    x = x + jnp.tanh(g_ffn[1]) * _L1_ffn_ref(_layernorm(x, axis=-1), L1_ffn_Wr, L1_ffn_br, L1_ffn_ln_g, L1_ffn_ln_b, L1_ffn_W1, L1_ffn_b1, L1_ffn_W2, L1_ffn_b2)
    return x

_drawn_inputs = setup_inputs


def setup_inputs(seed=0):
    import zlib

    import numpy as np

    out = dict(_drawn_inputs(seed))
    spreads = {'g_ffn': (-1.0, 0.6),
     'L0_xattn_ln_x_g': (1.0, 0.6),
     'L0_xattn_ln_x_b': (0.0, 0.8),
     'L0_xattn_ln_l_g': (1.0, 0.58),
     'L0_xattn_ln_l_b': (0.0, 0.1),
     'L0_xattn_q_gamma': (1.0, 0.6),
     'L0_xattn_k_gamma': (1.0, 0.6),
     'L0_xattn_b_out': (0.0, 0.1),
     'L1_xattn_bq': (0.0, 0.1),
     'L1_xattn_bk': (0.0, 2.0),
     'L1_xattn_bv': (0.0, 0.1),
     'L1_xattn_bo': (0.0, 0.1),
     'L1_xattn_ln_gamma': (1.0, 0.2),
     'L1_xattn_ln_beta': (0.0, 0.1),
     'L1_ffn_br': (0.0, 0.43),
     'L1_ffn_ln_g': (1.0, 0.6),
     'L1_ffn_ln_b': (0.0, 2.0),
     'L1_ffn_b1': (0.0, 0.8),
     'L1_ffn_b2': (0.0, 0.414)}
    factors = {}
    for name, (base, spread) in spreads.items():
        noise = np.random.default_rng([zlib.crc32(name.encode()), seed]).standard_normal(out[name].shape)
        drawn = base * np.exp(spread * noise) if base else spread * noise
        out[name] = jnp.asarray(drawn.astype(out[name].dtype))
    for name, factor in factors.items():
        out[name] = (out[name] * factor).astype(out[name].dtype)
    return out
```

```python
from contextlib import ExitStack

import numpy as np
import concourse.bass as bass
from concourse import mybir

F32 = mybir.dt.float32
F32R = mybir.dt.float32r
U8 = mybir.dt.uint8
U32 = mybir.dt.uint32
I32 = mybir.dt.int32
ALU = mybir.AluOpType
ACT = mybir.ActivationFunctionType
AX = mybir.AxisListType
ds = bass.ds

P = 128
B, S, D = 2, 1024, 256
KC = D // P
NT = B * S // P
GT = 4
GN = GT * P
NG = NT // GT
BG = NG // B
C = 77
H0, E0 = 4, 64
KEYS = S + C
KPAD = KEYS + 1
KT = S // P + 1
F = 1024
FC = F // P
H1 = 16
HK = H1 * C
HC = -(-HK // P)
E = 8
ROW = D + 4
GATE, TOKEN, MEAN, ROOT = D, D + 1, D + 2, D + 3
SLOTS = (B * S - E) // P + E
NO_TOKEN = 4096.0
LN_EPS = 1e-5
RMS_EPS = 1e-8
MASKED = 1e30


def spike_edges(steps=5, beta=0.9, threshold=1.0):
    f = np.float32

    def spikes(y):
        mem, count = f(0), 0
        for _ in range(steps):
            mem = f(f(f(beta) * mem) + y) - f(mem > threshold)
            count += int(mem > threshold)
        return count
    edges = []
    for n in range(1, steps + 1):
        lo, hi = f(0), f(4)
        while np.nextafter(lo, hi) < hi:
            mid = f((lo + hi) / 2)
            lo, hi = (mid, hi) if spikes(mid) < n else (lo, mid)
        edges.append(float(lo))
    return edges


class Ring:

    def __init__(self, eng, full, free, banks=8):
        self.eng, self.full, self.free, self.banks, self.n = eng, full, free, banks, 0

    def to_fill(self):
        if self.n >= self.banks:
            self.eng.wait_ge(self.free, self.n - self.banks + 1)
        return self.n % self.banks

    def filled(self, ins):
        ins.then_inc(self.full, 1)
        self.n += 1

    def to_read(self):
        self.eng.wait_ge(self.full, self.n + 1)
        return self.n % self.banks

    def read(self, ins):
        ins.then_inc(self.free, 1)
        self.n += 1


class Count:

    def __init__(self, eng, sem, base=0):
        self.eng, self.sem, self.base, self.n = eng, sem, base, 0

    def add(self, ins):
        self.n += 1
        return ins.then_inc(self.sem, 1)

    def wait(self):
        self.eng.wait_ge(self.sem, self.base + self.n)


def wait_apart(eng, sem, value, waited):
    eng.wait_ge(sem, value)
    eng.sem_inc(waited, 1)


def layers_kernel(nc, t):
    ctx = ExitStack()
    floats = {}

    def sb(where, name, shape, dt=F32):
        floats[id(where)] = floats.get(id(where), 0) + 8 * -(-int(np.prod(shape[1:])) // 8)
        return where.enter_context(nc.sbuf_tensor(name, shape, dt))
    sem = lambda name: ctx.enter_context(nc.semaphore(name))

    PS = ctx.enter_context(nc.psum_tensor("PS", [P, 8, 512], F32))
    PSf = PS[:].rearrange("p k n -> p (k n)")

    XR = sb(ctx, "XR", [P, NT, ROW])
    X = XR[:, :, 0:D]
    ident = sb(ctx, "ident", [P, P])
    onesr = sb(ctx, "onesr", [1, P], F32R)
    ones33 = sb(ctx, "ones33", [33, P], F32R)
    gates = sb(ctx, "gates", [P, 4])
    tg = sb(ctx, "tg", [P, 4])
    tg5 = sb(ctx, "tg5", [P, 1])
    minus_half = sb(ctx, "minus_half", [P, 32])
    ctxn = sb(ctx, "ctxn", [P, B, D])
    stats = sb(ctx, "stats", [P, NT + B, 6])
    meanvar = sb(ctx, "meanvar", [P, NT + B, 2])
    rs = sb(ctx, "rs", [P, 3, NT + B])
    rstd = sb(ctx, "rstd", [P, NT + B])
    Z = sb(ctx, "Z", [P, GT, D])

    stg = sb(ctx, "stg", [P, GT, 6])
    mvg = sb(ctx, "mvg", [P, GT, 2])
    rsg = sb(ctx, "rsg", [P, GT])
    bk1 = sb(ctx, "bk1", [P, FC])
    bv1 = sb(ctx, "bv1", [P, FC])
    LG = sb(ctx, "LG", [P, NT, E])
    fill = sb(ctx, "fill", [P, ROW])
    upper = sb(ctx, "upper", [P, P])
    onesq = sb(ctx, "onesq", [P, P])
    iotas = sb(ctx, "iotas", [P, 3, P])
    top = sb(ctx, "top", [P, NT, 8])
    topi = sb(ctx, "topi", [P, NT, 8], U32)
    RT = sb(ctx, "RT", [P, 10, NT, E])
    rti = sb(ctx, "rti", [P, SLOTS * E], I32)
    rtn = sb(ctx, "rtn", [P, 4, NT])
    slot = sb(ctx, "slot", [P, NT], U32)
    expert_of = sb(ctx, "expert_of", [P, SLOTS], I32)
    leg = sb(ctx, "leg", [P, KC])
    leb = sb(ctx, "leb", [P, KC])
    b1 = sb(ctx, "b1", [P, E, FC])

    att = ExitStack()
    QS = sb(att, "QS", [P, BG, H0, GN], F32R)
    KH = sb(att, "KH", [P, H0, KPAD], F32R)
    KL = sb(att, "KL", [P, H0, KPAD], F32R)
    V = sb(att, "V", [P, KT, D])
    prob = sb(att, "prob", [P, 2, GT, KEYS])
    probT = sb(att, "probT", [P, 2, GN])
    rms2 = sb(att, "rms2", [P, 2, 2 * H0])
    OT = sb(att, "OT", [E0, 2, GN])
    wqkv = sb(att, "wqkv", [P, KC, 3 * D])
    wout = sb(att, "wout", [E0, H0, D])
    boutb = sb(att, "boutb", [P, D])
    lnlg = sb(att, "lnlg", [P, KC])
    lnlb = sb(att, "lnlb", [P, KC])
    lnxg = sb(att, "lnxg", [P, KC])
    lnxb = sb(att, "lnxb", [P, KC])
    qgam = sb(att, "qgam", [P, 1])
    kgam = sb(att, "kgam", [P, 1])
    masku = sb(att, "masku", [1, B, C], U8)
    maskr = sb(att, "maskr", [1, B, C + 1], F32R)
    lnT = sb(att, "lnT", [P, KC, GN])
    sq = sb(att, "sq", [P, 2, 2 * D])
    ssum = sb(att, "ssum", [P, 2, 2 * H0])
    rrms = sb(att, "rrms", [P, 2, 2 * H0])
    qk2 = sb(att, "qk2", [P, 2, 2 * H0, 2, E0])
    nmax = sb(att, "nmax", [P, 2, GT])
    lsum = sb(att, "lsum", [P, 2, GT])
    rl = sb(att, "rl", [P, 2, GT])
    att.close()

    late = ExitStack()
    wqT = sb(late, "wqT", [P, FC, D])
    keysT = sb(late, "keysT", [P, FC, B, 2, C])
    valsT = sb(late, "valsT", [P, FC, B, C])
    ctxT = sb(late, "ctxT", [P, KC, B, C])
    vwn = sb(late, "vwn", [C, H1, D])
    bqz = sb(late, "bqz", [P, FC, 33])
    wfcT = sb(late, "wfcT", [P, KC, F])
    wprojT = sb(late, "wprojT", [P, FC, D])
    zT = sb(late, "zT", [P, KC, GN])
    relu = sb(late, "relu", [P, 2, GN])
    hT = sb(late, "hT", [P, FC, GN])
    wfc = hT[:, 0:FC // 2, :].rearrange("p a (b d) -> p (a b) d", d=D)
    wproj = hT[:, FC // 2:FC, :].rearrange("p (k a) n -> p k (a n)", k=KC)
    spikes = sb(late, "spikes", [P, GN])
    kw = sb(late, "kw", [P, KC, B, HK])
    kc = sb(late, "kc", [33, B, HK], F32R)
    vw = sb(late, "vw", [P, B, HC, D])
    late.close()

    moe = ExitStack()
    w1 = sb(moe, "w1", [P, E, KC, F])
    w2 = sb(moe, "w2", [P, E, FC, D])
    moe.close()

    BELOW = max(floats[id(r)] for r in (att, late, moe))
    above = ExitStack()
    above.enter_context(nc.sbuf_tensor("below", [P, BELOW], F32))
    wk1 = sb(above, "wk1", [P, KC, F])
    wv1 = sb(above, "wv1", [P, KC, F])
    wq1 = sb(above, "wq1", [P, KC, F])
    wo1 = sb(above, "wo1", [P, FC, D])
    above.close()
    above = ExitStack()
    above.enter_context(nc.sbuf_tensor("below2", [P, BELOW], F32))
    zc = sb(above, "zc", [P, 2, D])
    zbo = sb(above, "zbo", [P, 2, D])
    zcT = sb(above, "zcT", [P, 2, D])
    pc = sb(above, "pc", [P, 2, HK])
    pcT = sb(above, "pcT", [P, HC, P])
    resid = sb(above, "resid", [P, 2, D])
    x3 = sb(above, "x3", [P, 2, D])
    x3T = sb(above, "x3T", [P, 2, D])
    bob = sb(above, "bob", [P, D])
    lngb = sb(above, "lngb", [P, D])
    lnbb = sb(above, "lnbb", [P, D])
    mx1 = sb(above, "mx1", [P, 2, H1])
    sum1 = sb(above, "sum1", [P, 2, H1])
    st1 = sb(above, "st1", [P, 2, 2, 6])
    mv1 = sb(above, "mv1", [P, 2, 2, 2])
    rs1 = sb(above, "rs1", [P, 2, 2])
    wr = sb(above, "wr", [P, KC, E])
    brb = sb(above, "brb", [P, E])
    above.close()
    above = ExitStack()
    above.enter_context(nc.sbuf_tensor("below3", [P, BELOW], F32))
    xe = sb(above, "xe", [P, 4, ROW])
    ze = sb(above, "ze", [P, 2, D])
    xeT = sb(above, "xeT", [P, 2, KC, P])
    he = sb(above, "he", [P, 2, F])
    heT = sb(above, "heT", [P, FC, P])
    oe = sb(above, "oe", [P, 2, D])
    token = sb(above, "token", [P, 2], U32)
    b2 = sb(above, "b2", [1, E * D])
    ones = sb(above, "ones", [1, P])
    above.close()

    x_in = [sem(f"x_in{g}") for g in range(NG)]
    ctx_in, wts_in, vec_in = sem("ctx_in"), sem("wts_in"), sem("vec_in")
    ident_set, zero_set, half_set = sem("ident_set"), sem("zero_set"), sem("half_set")
    stats_ready, rstd_ready, ones_set, mask_set = sem("stats_ready"), sem("rstd_ready"), sem("ones_set"), sem("mask_set")
    wout_scaled, bias_added, gam_scaled = sem("wout_scaled"), sem("bias_added"), sem("gam_scaled")
    tanh_ready = sem("tanh_ready")
    z_ready, zT_done, lnT_ready = sem("z_ready"), sem("zT_done"), sem("lnT_ready")
    qkv_done, sq_ready, v_copied, ssum_ready, rrms_ready = (sem("qkv_done"), sem("sq_ready"), sem("v_copied"),
                                                           sem("ssum_ready"), sem("rrms_ready"))
    qk2_ready, qkT_done, high_ready, low_ready = sem("qk2_ready"), sem("qkT_done"), sem("high_ready"), sem("low_ready")
    s_done, max_ready, exp_done, t_done, probT_ready = (sem("s_done"), sem("max_ready"), sem("exp_done"),
                                                        sem("t_done"), sem("probT_ready"))
    pv_done, ot_ready, proj_done, rl_ready, proj_added = (sem("pv_done"), sem("ot_ready"), sem("proj_done"),
                                                          sem("rl_ready"), sem("proj_added"))
    dve_own, pool_own, act_own = sem("dve_own"), sem("pool_own"), sem("act_own")
    out_done = sem("out_done")

    rms_mean = sem("rms_mean")
    kept_in, fold_in, ffn_in, cross_in, b2_in = sem("kept_in"), sem("fold_in"), sem("ffn_in"), sem("cross_in"), sem("b2_in")
    fold_done, fold_read, zeroed, vwn_ready, vw_out, vw_in = (sem("fold_done"), sem("fold_read"), sem("zeroed"),
                                                              sem("vwn_ready"), [sem(f"vw_out{b}") for b in range(B)],
                                                              sem("vw_in"))
    wT_done, wT_ready = sem("wT_done"), sem("wT_ready")
    g_stats, g_rstd, g_z, g_zT, g_zT_ready = sem("g_stats"), sem("g_rstd"), sem("g_z"), sem("g_zT"), sem("g_zT_ready")
    h_done, relu_ready, h_ready, y_done, lif_done = (sem("h_done"), sem("relu_ready"), sem("h_ready"), sem("y_done"),
                                                     sem("lif_done"))
    c_stats, c_rstd, c_z, c_zb, c_zT, c_zT_ready = (sem("c_stats"), sem("c_rstd"), sem("c_z"), sem("c_zb"),
                                                    sem("c_zT"), sem("c_zT_ready"))
    sc_done, sc_read, pexp_ready, pnorm_ready, tp_done, tp_act, tp_dve = (
        sem("sc_done"), sem("sc_read"), sem("pexp_ready"), sem("pnorm_ready"), sem("tp_done"), sem("tp_act"),
        sem("tp_dve"))
    pvc_done, res_ready, r_stats, r_rstd, x3_ready, x3_copied, x3T_done, x3T_ready, lg_done, lg_ready = (
        sem("pvc_done"), sem("res_ready"), sem("r_stats"), sem("r_rstd"), sem("x3_ready"), sem("x3_copied"),
        sem("x3T_done"), sem("x3T_ready"), sem("lg_done"), sem("lg_ready"))
    const_set, fill_out, rank_done, oh_ready, gexp_ready, gexp_in, slot_ready, scattered = (
        sem("const_set"), sem("fill_out"), sem("rank_done"), sem("oh_ready"), sem("gexp_ready"), sem("gexp_in"),
        sem("slot_ready"), sem("scattered"))
    w1_in, w2_in = [sem(f"w1_in{e}") for e in range(1)], [sem(f"w2_in{e}") for e in range(1)]
    xe_in = [sem(f"xe_in{k}") for k in range(4)]
    e_stats, e_rstd, e_z, e_zT, e_zT_ready = sem("e_stats"), sem("e_rstd"), sem("e_z"), sem("e_zT"), sem("e_zT_ready")
    g1_done, he_act, he_dve, heT_done, heT_act, heT_dve, g2_done, oe_ready = (
        sem("g1_done"), sem("he_act"), sem("he_dve"), sem("heT_done"), sem("heT_act"), sem("heT_dve"),
        sem("g2_done"), sem("oe_ready"))
    x3_stats, x3_meanvar, x3_once, wr_summed = sem("x3_stats"), sem("x3_meanvar"), sem("x3_once"), sem("wr_summed")
    waited_pool, waited_dve = sem("waited_pool"), sem("waited_dve")
    out_rows = [sem(f"out_rows{k}") for k in range(2)]
    c_bn, c_max, c_sum, c_var, r_bn, r_own, r_var, x_beta, lnb_scaled = (
        sem("c_bn"), sem("c_max"), sem("c_sum"), sem("c_var"), sem("r_bn"), sem("r_own"), sem("r_var"), sem("x_beta"),
        sem("lnb_scaled"))
    route_own, expert_ready, e_bn, e_var, e_token, ones1_set = (sem("route_own"), sem("expert_ready"), sem("e_bn"),
                                                               sem("e_var"), sem("e_token"), sem("ones1_set"))
    bqz_in, kc_high, rsg_var, g_bn, lif_step, tg_ready = (sem("bqz_in"), sem("kc_high"), sem("rsg_var"), sem("g_bn"),
                                                          sem("lif_step"), sem("tg_ready"))

    VECS = 17
    ITEMS = S // P + 1
    UNITS = BG + 1
    LAST = ITEMS - 1
    MP = BG * H0
    CHUNKS = [(0, 512), (512, 1024), (1024, KPAD)]
    key_rows = lambda j: P if j < KT - 1 else C

    def dve_norm(dve):
        own = Count(dve, dve_own)
        for g in range(NG):
            dve.wait_ge(x_in[g], 16)
            for i in range(GT * g, GT * g + GT):
                own.add(dve.bn_stats(stats[:, i, :], X[:, i, :]))
        dve.wait_ge(ctx_in, 16)
        for b in range(B):
            own.add(dve.bn_stats(stats[:, NT + b, :], ctxn[:, b, :]))
        own.wait()
        for i in range(NT + B):
            last = dve.bn_aggr(meanvar[:, i, :], stats[:, i, :])
        last.then_inc(stats_ready, 1)

    def pool_norm(pool):
        own = Count(pool, pool_own)
        pool.wait_ge(half_set, 1)
        pool.wait_ge(stats_ready, 1)
        var, once, twice = meanvar[:, :, 1], rs[:, 0, :], rs[:, 1, :]
        root = minus_half[:, 0:NT + B]
        for ins in (lambda: pool.tensor_scalar(once, var, LN_EPS, None, ALU.add),
                    lambda: pool.tensor_tensor(once, once, root, ALU.pow),
                    lambda: pool.tensor_tensor(twice, var, once, ALU.mult),
                    lambda: pool.tensor_tensor(twice, twice, once, ALU.mult),
                    lambda: pool.tensor_scalar(twice, twice, LN_EPS, None, ALU.add),
                    lambda: pool.tensor_tensor(twice, twice, root, ALU.pow)):
            own.add(ins())
            own.wait()
        pool.tensor_tensor(rstd[:, 0:NT], once[:, 0:NT], twice[:, 0:NT], ALU.mult).then_inc(rstd_ready, 1)
        pool.tensor_copy(rstd[:, NT:NT + B], once[:, NT:NT + B]).then_inc(rstd_ready, 1)

    def normalize(dve, b, u):
        if u > 0:
            dve.wait_ge(zT_done, UNITS * b + u)
        for s in range(GT if u < BG else 1):
            row = X[:, b * (S // P) + GT * u + s, :] if u < BG else ctxn[:, b, :]
            at = b * (S // P) + GT * u + s if u < BG else b + NT
            last = dve.tensor_scalar(Z[:, s, :], row, meanvar[:, at, 0:1], rstd[:, ds(at, 1)],
                                     ALU.subtract, ALU.mult)
        last.then_inc(z_ready, 1)

    def dve_project(dve, b):
        item = lambda i: b * ITEMS + i
        normalize(dve, b, 0)
        for i in range(ITEMS + 1):
            p = i % 2
            if i < ITEMS:
                dve.wait_ge(sq_ready, item(i) + 1)
                dve.tensor_reduce(ssum[:, p, :], sq[:, p, :].rearrange("p (h e) -> p h e", e=E0), AX.X, ALU.add) \
                   .then_inc(ssum_ready, 1)
            if i >= 1:
                j, s = i - 1, (i - 1) % GT
                dve.wait_ge(high_ready, item(j) + 1)
                if j < LAST:
                    low = QS[E0:P, j // GT, :, s * P:s * P + P]
                    dve.scalar_tensor_tensor(low, PS[E0:P, 6, :].rearrange("p (h n) -> p h n", h=H0), qgam[E0:P, :],
                                             low.bitcast(F32), ALU.mult, ALU.subtract)
                w = P if j < LAST else C + 1
                cols = slice(j * P, j * P + w)
                dve.scalar_tensor_tensor(KL[:, :, cols], PS[:, 7, :].rearrange("p (h n) -> p h n", h=H0)[:, :, 0:w],
                                         kgam[:, :], KH[:, :, cols].bitcast(F32), ALU.mult, ALU.subtract) \
                   .then_inc(low_ready, 1)
            if i < ITEMS:
                dve.wait_ge(rrms_ready, item(i) + 1)
                h = 2 * H0
                rows = PS[:, 2 + 2 * p, :].rearrange("p (h e) -> p h e", e=E0)
                dve.tensor_tensor(qk2[:, p, :, :, :], rows.unsqueeze(2).to_broadcast([P, h, 2, E0]),
                                  rrms[:, p, :].unsqueeze(2).unsqueeze(3).to_broadcast([P, h, 2, E0]), ALU.mult) \
                   .then_inc(qk2_ready, 1)
            if i == 0 or i == GT:
                normalize(dve, b, 1 + i // GT)

    def act_project(act, b):
        item = lambda i: b * ITEMS + i

        def scale_rows(u):
            act.wait_ge(zT_done, UNITS * b + u + 1)
            n, g, c = (GN, lnlg, lnlb) if u < BG else (P, lnxg, lnxb)
            for k in range(KC):
                last = act.activation(lnT[:, k, 0:n], PS[:, k, 0:n], ACT.Identity, bias=c[:, k:k + 1],
                                      scale=g[:, k:k + 1])
            last.then_inc(lnT_ready, 1)

        scale_rows(0)
        for i in range(ITEMS + 1):
            p = i % 2
            if i < ITEMS:
                act.wait_ge(qkv_done, item(i) + 1)
                act.activation(sq[:, p, :], PS[:, 2 + 2 * p, :], ACT.Square).then_inc(sq_ready, 1)
                act.activation(V[:, i, :], PS[:, 3 + 2 * p, 0:D], ACT.Copy).then_inc(v_copied, 1)
            if i == 3:
                scale_rows(1)
            if i == 7:
                scale_rows(2)
            if i >= 1:
                j, s = i - 1, (i - 1) % GT
                act.wait_ge(qkT_done, item(j) + 1)
                if j < LAST:
                    act.activation(QS[:, j // GT, :, s * P:s * P + P], PS[:, 6, :].rearrange("p (h n) -> p h n", h=H0),
                                   ACT.Copy, scale=qgam[:, :])
                w = P if j < LAST else C + 1
                act.activation(KH[:, :, j * P:j * P + w],
                               PS[:, 7, :].rearrange("p (h n) -> p h n", h=H0)[:, :, 0:w],
                               ACT.Copy, scale=kgam[:, :]).then_inc(high_ready, 1)

    def pool_project(pool, b):
        for i in range(ITEMS):
            p = i % 2
            wait_apart(pool, ssum_ready, b * ITEMS + i + 1, waited_pool)
            pool.tensor_scalar(rms2[:, p, :], ssum[:, p, :], 1.0 / E0, RMS_EPS ** 2, ALU.mult, ALU.max) \
                .then_inc(rms_mean, 1)
            pool.wait_ge(rms_mean, b * ITEMS + i + 1)
            pool.tensor_tensor(rrms[:, p, :], rms2[:, p, :], minus_half[:, 0:2 * H0], ALU.pow).then_inc(rrms_ready, 1)
            if i % GT == 1 and i < LAST:
                g = i // GT
                wait_apart(pool, z_ready, UNITS * b + g + 1, waited_pool)
                for s in range(GT):
                    row = X[:, b * (S // P) + GT * g + s, :]
                    last = pool.tensor_tensor(row, row, boutb[:], ALU.add)
                last.then_inc(bias_added, 1)

    def pe_project(pe, b):
        item = lambda i: b * ITEMS + i

        def turn_rows(u):
            pe.wait_ge(z_ready, UNITS * b + u + 1)
            if u > 0:
                pe.wait_ge(lnT_ready, UNITS * b + u)
            for s in range(GT if u < BG else 1):
                for k in range(KC):
                    last = pe.transpose(PS[:, k, s * P:s * P + P], Z[:, s, k * P:k * P + P], ident[:])
            last.then_inc(zT_done, 1)

        def qkv(i):
            s, p = i % GT, i % 2
            pe.wait_ge(lnT_ready, UNITS * b + i // GT + 1)
            if i >= 2:
                pe.wait_ge(qk2_ready, item(i) - 1)
                pe.wait_ge(v_copied, item(i) - 1)
            for c0, c1, bank in ((0, 2 * D, 2 + 2 * p), (2 * D, 3 * D, 3 + 2 * p)):
                for k in range(KC):
                    last = pe.matmul(PS[:, bank, 0:c1 - c0], lnT[:, k, s * P:s * P + P], wqkv[:, k, c0:c1],
                                     start=k == 0, stop=k == KC - 1)
            last.then_inc(qkv_done, 1)

        def turn_heads(i):
            pe.wait_ge(qk2_ready, item(i) + 1)
            if i >= 1:
                pe.wait_ge(low_ready, item(i))
            for h in range(0 if i < LAST else H0, 2 * H0):
                last = pe.transpose(PS[:, 6 + h // H0, (h % H0) * P:(h % H0) * P + P],
                                    qk2[:, i % 2, h, :, :].rearrange("p a e -> p (a e)"), ident[:])
            last.then_inc(qkT_done, 1)

        turn_rows(0)
        for i in range(ITEMS + 1):
            if i < ITEMS:
                qkv(i)
            if i == 3 or i == 7:
                turn_rows(1 + i // GT)
            if i >= 1:
                turn_heads(i - 1)

    def pe_attend(pe, b):
        def scores(m, s):
            g, h = m // H0, m % H0
            at = GT * m + s
            if at >= 2:
                pe.wait_ge(exp_done, GT * MP * b + at - 1)
            elif at == 0:
                pe.wait_ge(low_ready, ITEMS * b + ITEMS)
                pe.wait_ge(v_copied, ITEMS * b + ITEMS)
            k0 = 3 * (at % 2)
            q = QS[:, g, h, s * P:s * P + P]
            for c, (c0, c1) in enumerate(CHUNKS):
                pe.matmul(PS[:, k0 + c, 0:c1 - c0], q, KH[:, h, c0:c1], start=True, stop=False)
            for c, (c0, c1) in enumerate(CHUNKS):
                last = pe.matmul(PS[:, k0 + c, 0:c1 - c0], q, KL[:, h, c0:c1], start=False, stop=c < 2)
            last = pe.matmul(PS[:, k0 + 2, 0:C + 1], onesr[:], maskr[0:1, b, :], start=False, stop=True)
            last.then_inc(s_done, 1)

        def turn_probs(m, j):
            n = MP * b + m
            if j == 0:
                pe.wait_ge(exp_done, GT * n + GT)
            if m > 0 or j > 0:
                pe.wait_ge(probT_ready, KT * n + j)
            for s in range(GT):
                last = pe.transpose(PS[0:key_rows(j), 6, s * P:s * P + P],
                                    prob[:, m % 2, s, j * P:j * P + key_rows(j)], ident[:])
            last.then_inc(t_done, 1)

        def values(m, j):
            n, h, r = MP * b + m, m % H0, key_rows(j)
            pe.wait_ge(probT_ready, KT * n + j + 1)
            if j == 0 and m > 0:
                pe.wait_ge(proj_added, 2 * n)
            ins = pe.matmul(PS[0:E0, 7, :], V[0:r, j, h * E0:h * E0 + E0], probT[0:r, j % 2, :],
                            start=j == 0, stop=j == KT - 1)
            if j == KT - 1:
                ins.then_inc(pv_done, 1)

        def project_out(m, half):
            n, h = MP * b + m, m % H0
            if half == 0:
                pe.wait_ge(ot_ready, n + 1)
                pe.wait_ge(wout_scaled, 1)
            else:
                pe.wait_ge(proj_added, 2 * n + 1)
            for s in range(2):
                c = (2 * half + s) * P
                last = pe.matmul(PS[:, 7, s * D:s * D + D], OT[:, m % 2, c:c + P], wout[:, h, :],
                                 start=True, stop=True)
            last.then_inc(proj_done, 1)

        for s in range(GT):
            scores(0, s)
        for m in range(MP):
            nxt = (lambda s: scores(m + 1, s)) if m + 1 < MP else (lambda s: None)
            prev = (lambda half: project_out(m - 1, half)) if m > 0 else (lambda half: None)
            turn_probs(m, 0)
            prev(0)
            nxt(0)
            prev(1)
            turn_probs(m, 1)
            nxt(1)
            values(m, 0)
            turn_probs(m, 2)
            values(m, 1)
            nxt(2)
            turn_probs(m, 3)
            values(m, 2)
            turn_probs(m, 4)
            values(m, 3)
            nxt(3)
            for j in range(5, KT):
                turn_probs(m, j)
                values(m, j - 1)
            values(m, KT - 1)
        project_out(MP - 1, 0)
        project_out(MP - 1, 1)

    def dve_attend(dve, b):
        def row_max(m, s):
            k0 = 3 * ((GT * m + s) % 2)
            dve.wait_ge(s_done, GT * (MP * b + m) + s + 1)
            dve.tensor_reduce(nmax[:, m % 2, s:s + 1], PSf[:, 512 * k0:512 * k0 + KEYS], AX.X, ALU.max, negate=True) \
               .then_inc(max_ready, 1)

        def copy_probs(m, j):
            dve.wait_ge(t_done, KT * (MP * b + m) + j + 1)
            r = key_rows(j)
            dve.tensor_copy(probT[0:r, j % 2, :], PS[0:r, 6, :]).then_inc(probT_ready, 1)

        def reciprocals(m):
            dve.wait_ge(exp_done, GT * (MP * b + m) + GT)
            dve.reciprocal(rl[:, m % 2, :], lsum[:, m % 2, :]).then_inc(rl_ready, 1)

        def add_out(m, half):
            n, g = MP * b + m, m // H0
            dve.wait_ge(proj_done, 2 * n + half + 1)
            if half == 0:
                dve.wait_ge(rl_ready, n + 1)
                if m % H0 == 0:
                    dve.wait_ge(bias_added, BG * b + g + 1)
                else:
                    dve.wait_ge(proj_added, 2 * n)
            for s in range(2):
                row = X[:, b * (S // P) + GT * g + 2 * half + s, :]
                last = dve.scalar_tensor_tensor(row, PS[:, 7, s * D:s * D + D], rl[:, m % 2, 2 * half + s:2 * half + s + 1],
                                                row, ALU.mult, ALU.add)
            last.then_inc(proj_added, 1)

        for s in range(GT):
            row_max(0, s)
        for m in range(MP):
            nxt = (lambda s: row_max(m + 1, s)) if m + 1 < MP else (lambda s: None)
            copy_probs(m, 0)
            if m > 0:
                add_out(m - 1, 0)
            nxt(0)
            if m > 0:
                add_out(m - 1, 1)
            nxt(1)
            copy_probs(m, 2)
            nxt(2)
            copy_probs(m, 4)
            nxt(3)
            copy_probs(m, 6)
            reciprocals(m)
            copy_probs(m, 8)
        add_out(MP - 1, 0)
        add_out(MP - 1, 1)

    def act_attend(act, b):
        def exps(m, s):
            k0 = 3 * ((GT * m + s) % 2)
            act.wait_ge(max_ready, GT * (MP * b + m) + s + 1)
            act.activation(prob[:, m % 2, s, :], PSf[:, 512 * k0:512 * k0 + KEYS], ACT.Exp,
                           bias=nmax[:, m % 2, s:s + 1], accum_out=lsum[:, m % 2, s:s + 1]).then_inc(exp_done, 1)

        def copy_probs(m, j):
            act.wait_ge(t_done, KT * (MP * b + m) + j + 1)
            act.activation(probT[:, j % 2, :], PS[:, 6, :], ACT.Copy).then_inc(probT_ready, 1)

        for s in range(GT):
            exps(0, s)
        for m in range(MP):
            nxt = (lambda s: exps(m + 1, s)) if m + 1 < MP else (lambda s: None)
            nxt(0)
            copy_probs(m, 1)
            nxt(1)
            copy_probs(m, 3)
            nxt(2)
            copy_probs(m, 5)
            nxt(3)
            copy_probs(m, 7)
            act.wait_ge(pv_done, MP * b + m + 1)
            act.activation(OT[:, m % 2, :], PS[0:E0, 7, :], ACT.Copy).then_inc(ot_ready, 1)

    ctx_chunks = [(c0, min(c0 + P, HK)) for c0 in range(0, HK, P)]

    def pe_fold(pe):
        bank = Ring(pe, fold_done, fold_read)
        pe.wait_ge(proj_added, 2 * MP * B)
        pe.wait_ge(ctx_in, 16)
        pe.wait_ge(fold_in, 16 * 4)
        k0 = bank.to_fill()
        for k in range(KC):
            for b in range(B):
                last = pe.transpose(PS[:, k0, (k * B + b) * P:(k * B + b) * P + P], ctxn[:, b, k * P:k * P + P], ident[:])
        bank.filled(last)
        for c2 in range(0, FC, 2):
            k0 = bank.to_fill()
            for c in range(2):
                for k in range(KC):
                    at = (c * KC + k) * P
                    last = pe.transpose(PS[:, k0, at:at + P], wq1[:, k, (c2 + c) * P:(c2 + c) * P + P], ident[:])
            bank.filled(last)
        pe.wait_ge(fold_read, 1)
        for w in (wk1, wv1):
            for c in range(FC):
                k0 = bank.to_fill()
                for k in range(KC):
                    last = pe.matmul(PS[:, k0, 0:B * C], w[:, k, c * P:c * P + P],
                                     ctxT[:, k, :, :].rearrange("p b c -> p (b c)"), start=k == 0, stop=k == KC - 1)
                bank.filled(last)
        pe.wait_ge(zeroed, 2)
        pe.wait_ge(bqz_in, 32)
        for c in range(FC):
            rhs = keysT[:, c, :, :, :].rearrange("p b a c -> p (b a c)")
            pe.wait_ge(fold_read, 1 + FC // 2 + c + 1)
            for k in range(KC):
                k0 = bank.to_fill()
                bank.filled(pe.matmul(PS[:, k0, 0:2 * B * C], wqT[:, c, k * P:k * P + P], rhs, start=True, stop=True))
            k0 = bank.to_fill()
            bank.filled(pe.matmul(PS[0:33, k0, 0:2 * B * C], bqz[:, c, :], rhs, start=True, stop=True))

        def values_times_wo(b):
            for h in range(H1):
                k0, c, lo = bank.to_fill(), h // 2, slice(h % 2 * E0, h % 2 * E0 + E0)
                bank.filled(pe.matmul(PS[0:C, k0, 0:D], valsT[lo, c, b, :], wo1[lo, c, :], start=True, stop=True))
        pe.wait_ge(fold_read, 1 + FC // 2 + 2 * FC)
        values_times_wo(0)
        pe.wait_ge(ffn_in, 32)
        for k in range(KC):
            for c4 in range(0, FC, 4):
                k0 = bank.to_fill()
                for c in range(4):
                    last = pe.transpose(PS[:, k0, c * P:c * P + P], wfc[:, c4 + c, k * P:k * P + P], ident[:])
                bank.filled(last)
        for c2 in range(0, FC, 2):
            k0 = bank.to_fill()
            for c in range(2):
                for k in range(KC):
                    at = (c * KC + k) * P
                    last = pe.transpose(PS[:, k0, at:at + P], wproj[:, k, (c2 + c) * P:(c2 + c) * P + P], ident[:])
            bank.filled(last)
        values_times_wo(1)

    def dve_fold(dve):
        bank = Ring(dve, fold_done, fold_read)
        dve.wait_ge(proj_added, 2 * MP * B)
        dve.wait_ge(pv_done, MP * B)
        dve.memset(keysT[:].rearrange("p c b a n -> p (c b a n)"), 0.0).then_inc(zeroed, 1)
        k0 = bank.to_read()
        bank.read(dve.tensor_copy(ctxT[:].rearrange("p k b c -> p (k b) c"),
                                  PS[:, k0, :].rearrange("p (a n) -> p a n", n=P)[:, :, 0:C]))
        for c2 in range(0, FC, 2):
            k0 = bank.to_read()
            bank.read(dve.tensor_copy(wqT[:, c2:c2 + 2, :], PS[:, k0, :].rearrange("p (c n) -> p c n", c=2)))
        dve.wait_ge(zeroed, 1)
        for c in range(FC):
            k0 = bank.to_read()
            for a in range(2):
                lo = slice(a * E0, a * E0 + E0)
                last = dve.tensor_scalar(keysT[lo, c, :, a, :], PS[lo, k0, 0:B * C].rearrange("p (b c) -> p b c", b=B),
                                         bk1[lo, c:c + 1], E0 ** -0.5, ALU.add, ALU.mult)
            bank.read(last)
        for c in range(FC):
            k0 = bank.to_read()
            bank.read(dve.tensor_scalar(valsT[:, c, :, :], PS[:, k0, 0:B * C].rearrange("p (b c) -> p b c", b=B),
                                        bv1[:, c:c + 1], None, ALU.add))
        for c in range(FC):
            cols = slice(2 * C * c, 2 * C * c + 2 * C)
            for k in range(KC):
                k0 = bank.to_read()
                bank.read(dve.tensor_copy(kw[:, k, :, cols], PS[:, k0, 0:2 * B * C].rearrange("p (b n) -> p b n", b=B)))
            k0 = bank.to_read()
            sums = PS[:, k0, 0:2 * B * C].rearrange("p (b n) -> p b n", b=B)
            dve.tensor_copy(kc[:, :, cols], sums[0:33]).then_inc(kc_high, 1)
            dve.wait_ge(kc_high, c + 1)
            bank.read(dve.tensor_tensor(kc[32:33, :, cols], sums[32:33], kc[32:33, :, cols].bitcast(F32), ALU.subtract))

        def copy_vwn(b):
            if b > 0:
                dve.wait_ge(vw_out[b - 1], 16)
            for h in range(H1):
                k0 = bank.to_read()
                bank.read(dve.tensor_copy(vwn[:, h, :], PS[0:C, k0, 0:D]))
        copy_vwn(0)
        for k in range(KC):
            for c4 in range(0, FC, 4):
                k0 = bank.to_read()
                bank.read(dve.tensor_copy(wfcT[:, k, c4 * P:c4 * P + 4 * P], PS[:, k0, :]))
        for c2 in range(0, FC, 2):
            k0 = bank.to_read()
            bank.read(dve.tensor_copy(wprojT[:, c2:c2 + 2, :], PS[:, k0, :].rearrange("p (c n) -> p c n", c=2)))
        copy_vwn(1)

    FOLD_VWN = [1 + FC // 2 + 2 * FC + 3 * FC + H1, 1 + FC // 2 + 2 * FC + 3 * FC + H1 + FC + H1]
    FOLD_ALL = FOLD_VWN[1]

    def sp_fold(sp):
        sp.wait_ge(proj_added, 2 * MP * B)
        sp.dma_start(wfc, t["L0_ffn_W_fc"].rearrange("(c p) d -> p c d", p=P)).then_inc(ffn_in, 16)
        sp.dma_start(wproj, t["L0_ffn_W_proj"].rearrange("(k p) f -> p k f", p=P)).then_inc(ffn_in, 16)
        sp.wait_ge(zeroed, 2)
        bq = t["L1_xattn_bq"].rearrange("(c p) -> p c", p=P).unsqueeze(2)
        for col in (0, 32):
            sp.dma_start(bqz[:, :, col:col + 1], bq, allow_slow_non_contiguous=True).then_inc(bqz_in, 16)
        for b in range(B):
            sp.wait_ge(fold_read, FOLD_VWN[b])
            rows = t["vw_rows"][b]
            sp.dma_start(rows.rearrange("(h c) n -> c h n", c=C), vwn[:]).then_inc(vw_out[b], 16)
            sp.wait_ge(vw_out[b], 16)
            whole = HK // P
            sp.dma_start(vw[:, b, 0:whole, :], rows[0:whole * P, :].rearrange("(t p) n -> p t n", p=P)).then_inc(vw_in, 16)
            sp.dma_start(vw[0:HK - whole * P, b, whole, :], rows[whole * P:HK, :]).then_inc(vw_in, 16)

    EDGES = spike_edges()

    def pe_ffn(pe):
        def turn(g):
            pe.wait_ge(g_z, g + 1)
            for s in range(GT):
                for k in range(KC):
                    last = pe.transpose(PS[:, k, s * P:s * P + P], Z[:, s, k * P:k * P + P], ident[:])
            last.then_inc(g_zT, 1)

        def group(g, last_group):
            pe.wait_ge(g_zT_ready, g + 1)
            for c in range(FC):
                if c >= 2:
                    pe.wait_ge(relu_ready, FC * g + c - 1)
                for k in range(KC):
                    last = pe.matmul(PS[:, 2 + c % 2, :], wfcT[:, k, c * P:c * P + P], zT[:, k, :],
                                     start=k == 0, stop=k == KC - 1)
                last.then_inc(h_done, 1)
            if not last_group:
                turn(g + 1)
            pe.wait_ge(h_ready, FC * g + FC)
            pe.wait_ge(lif_done, 2 * g + 1)
            for half in range(2):
                if half == 1:
                    pe.wait_ge(lif_done, 2 * g + 2)
                for s in range(2):
                    at = (2 * half + s) * P
                    for c in range(FC):
                        last = pe.matmul(PS[:, 4 + half, s * D:s * D + D], hT[:, c, at:at + P], wprojT[:, c, :],
                                         start=c == 0, stop=c == FC - 1)
                last.then_inc(y_done, 1)
        pe.wait_ge(fold_read, FOLD_ALL)
        turn(0)
        with pe.Fori(0, NG - 1) as g:
            group(g, False)
        group(NG - 1, True)

    def act_ffn(act):
        def copy_turned(g):
            act.wait_ge(g_zT, g + 1)
            for k in range(KC):
                last = act.activation(zT[:, k, :], PS[:, k, :], ACT.Copy)
            last.then_inc(g_zT_ready, 1)

        def group(g, last_group):
            for c in range(FC):
                act.wait_ge(h_done, FC * g + c + 1)
                act.activation(relu[:, c % 2, :], PS[:, 2 + c % 2, :], ACT.Relu).then_inc(relu_ready, 1)
                if c == 0:
                    act.wait_ge(y_done, 2 * g + 1)
                act.wait_ge(relu_ready, FC * g + c + 1)
                act.activation(hT[:, c, :], relu[:, c % 2, :], ACT.Square).then_inc(h_ready, 1)
            if not last_group:
                copy_turned(g + 1)
        copy_turned(0)
        with act.Fori(0, NG - 1) as g:
            group(g, False)
        group(NG - 1, True)

    def pool_ffn(pool):
        with pool.Fori(0, NG) as g:
            wait_apart(pool, g_stats, g + 1, waited_pool)
            pool.tensor_scalar(rsg[:], mvg[:, :, 1], LN_EPS, None, ALU.add).then_inc(rsg_var, 1)
            pool.wait_ge(rsg_var, g + 1)
            pool.tensor_tensor(rsg[:], rsg[:], minus_half[:, 0:GT], ALU.pow).then_inc(g_rstd, 1)

    def dve_ffn(dve):
        def norm(g):
            for s in range(GT):
                last = dve.bn_stats(stg[:, s, :], X[:, GT * g + s, :])
            last.then_inc(g_bn, 1)
            wait_apart(dve, g_bn, g + 1, waited_dve)
            for s in range(GT):
                last = dve.bn_aggr(mvg[:, s, :], stg[:, s, :])
            last.then_inc(g_stats, 1)
            dve.wait_ge(g_rstd, g + 1)
            for s in range(GT):
                last = dve.tensor_scalar(Z[:, s, :], X[:, GT * g + s, :], mvg[:, s, 0:1], rsg[:, s:s + 1],
                                         ALU.subtract, ALU.mult)
            last.then_inc(g_z, 1)

        def spike(g):
            for half in range(2):
                dve.wait_ge(y_done, 2 * g + half + 2)
                dve.wait_ge(lif_done, 2 * g + half + 2)
                y = PS[:, 4 + half, :]
                dve.tensor_scalar(spikes[:], y, EDGES[0], None, ALU.is_gt).then_inc(lif_step, 1)
                for n, edge in enumerate(EDGES[1:]):
                    dve.wait_ge(lif_step, 5 * (2 * g + half) + n + 1)
                    last = dve.scalar_tensor_tensor(spikes[:], y, edge, spikes[:], ALU.is_gt, ALU.add)
                    last.then_inc(lif_step, 1)
                dve.wait_ge(lif_step, 5 * (2 * g + half) + 5)
                x2 = X[:, ds(GT * g + 2 * half, 2), :]
                dve.scalar_tensor_tensor(x2, spikes[:].rearrange("p (s d) -> p s d", d=D), tg5[:], x2,
                                         ALU.mult, ALU.add).then_inc(lif_done, 1)
        norm(0)
        with dve.Fori(0, NG - 1) as g:
            dve.wait_ge(g_zT, g + 1)
            norm(g + 1)
            spike(g)
        spike(NG - 1)

    SCORES = [(c0, min(c0 + 512, HK)) for c0 in range(0, HK, 512)]
    TB = S // P
    PAIRS = TB // 2

    def pairs(eng, body):
        for b in range(B):
            for p in range(2):
                body(b, TB * b + p, p, b == 0 and p == 0, False)
            with eng.Fori(1, PAIRS - 1) as i:
                for p in range(2):
                    body(b, i * 2 + (TB * b + p), p, False, False)
            for p in range(2):
                body(b, TB * b + TB - 2 + p, p, False, b == B - 1 and p == 1)

    def pe_cross(pe):
        def turn(n, p, first):
            pe.wait_ge(c_z, n + 1)
            if not first:
                pe.wait_ge(c_zT_ready, n)
            for k in range(KC):
                last = pe.transpose(PS[:, 0, k * P:k * P + P], zc[:, p, k * P:k * P + P], ident[:])
            last.then_inc(c_zT, 1)

        def scores(n, b, p, first):
            pe.wait_ge(c_zT_ready, n + 1)
            if not first:
                pe.wait_ge(sc_read, n)
            for i, (c0, c1) in enumerate(SCORES):
                for k in range(KC):
                    pe.matmul(PS[:, 1 + i, 0:c1 - c0], zcT[:, p, k * P:k * P + P], kw[:, k, b, c0:c1],
                              start=k == 0, stop=False)
                last = pe.matmul(PS[:, 1 + i, 0:c1 - c0], ones33[:], kc[:, b, c0:c1], start=False, stop=True)
            last.then_inc(sc_done, 1)

        def turn_x3(n, p):
            pe.wait_ge(x3_copied, n + 1)
            for k in range(KC):
                last = pe.transpose(PS[:, 7, D + k * P:D + k * P + P], x3[:, p, k * P:k * P + P], ident[:])
            last.then_inc(x3T_done, 1)

        def logits(n, p):
            pe.wait_ge(x3T_ready, n + 1)
            for k in range(KC):
                last = pe.matmul(PS[:, 7, 0:E], x3T[:, p, k * P:k * P + P], wr[:, k, :], start=k == 0, stop=k == KC - 1)
            last.then_inc(lg_done, 1)

        def body(b, n, p, first, last_tile):
            if not last_tile:
                nb = b if not isinstance(n, int) else (n + 1) // TB
                turn(n + 1, 1 - p, False)
                scores(n + 1, nb, 1 - p, False)
            if not first:
                turn_x3(n - 1, 1 - p)
            pe.wait_ge(pnorm_ready, n + 1)
            for c, (c0, c1) in enumerate(ctx_chunks):
                ins = pe.transpose(PS[0:c1 - c0, 4 + c // 4, c % 4 * P:c % 4 * P + P], pc[:, p, c0:c1], ident[:])
            ins.then_inc(tp_done, 1)
            if not first:
                logits(n - 1, 1 - p)
                pe.wait_ge(lg_ready, n)
            pe.wait_ge(tp_act, 2 * n + 2)
            pe.wait_ge(tp_dve, 2 * n + 2)
            for c, (c0, c1) in enumerate(ctx_chunks):
                r = c1 - c0
                ins = pe.matmul(PS[:, 7, 0:D], pcT[0:r, c, :], vw[0:r, b, c, :], start=c == 0, stop=c == HC - 1)
            ins.then_inc(pvc_done, 1)

        pe.wait_ge(lif_done, 2 * NG + 2)
        pe.wait_ge(vw_in, 16 * 2 * B)
        pe.wait_ge(cross_in, 16 * CROSS_LOADS)
        turn(0, 0, True)
        scores(0, 0, 0, True)
        pairs(pe, body)
        turn_x3(NT - 1, 1)
        logits(NT - 1, 1)

    def dve_cross(dve):
        def norm(n, p, first=False):
            dve.bn_stats(st1[:, 0, p, :], X[:, n, :]).then_inc(c_bn, 1)
            wait_apart(dve, c_bn, n + 1, waited_dve)
            dve.bn_aggr(mv1[:, 0, p, :], st1[:, 0, p, :]).then_inc(c_stats, 1)
            dve.wait_ge(c_rstd, n + 1)
            if not first:
                dve.wait_ge(c_zT, n)
            dve.tensor_scalar(zc[:, p, :], X[:, n, :], mv1[:, 0, p, 0:1], rs1[:, 0, p:p + 1],
                              ALU.subtract, ALU.mult).then_inc(c_z, 1)

        def probs(n, p):
            sc = PSf[:, 512:512 + HK].rearrange("p (h c) -> p h c", c=C)
            pr = pc[:, p, :].rearrange("p (h c) -> p h c", c=C)
            by_head = lambda v: v[:, p, :].unsqueeze(2).to_broadcast([P, H1, C])
            dve.wait_ge(sc_done, n + 1)
            dve.tensor_reduce(mx1[:, p, :], sc, AX.X, ALU.max).then_inc(c_max, 1)
            dve.wait_ge(c_max, n + 1)
            dve.tensor_tensor(pr, sc, by_head(mx1), ALU.subtract).then_inc(sc_read, 1)

        def normalize_probs(n, p):
            pr = pc[:, p, :].rearrange("p (h c) -> p h c", c=C)
            by_head = lambda v: v[:, p, :].unsqueeze(2).to_broadcast([P, H1, C])
            dve.wait_ge(pexp_ready, n + 1)
            dve.tensor_reduce(sum1[:, p, :], pr, AX.X, ALU.add).then_inc(c_sum, 1)
            dve.wait_ge(c_sum, 2 * n + 1)
            dve.reciprocal(sum1[:, p, :], sum1[:, p, :]).then_inc(c_sum, 1)
            dve.wait_ge(c_sum, 2 * n + 2)
            dve.tensor_tensor(pr, pr, by_head(sum1), ALU.mult).then_inc(pnorm_ready, 1)

        def logits(n):
            dve.wait_ge(lg_done, n + 1)
            dve.tensor_copy(LG[:, n, :], PS[:, 7, 0:E]).then_inc(lg_ready, 1)
            dve.bn_stats(stats[:, n, :], X[:, n, :]).then_inc(x3_stats, 1)

        def finish(n, p):
            dve.wait_ge(pvc_done, n + 1)
            dve.wait_ge(c_zb, n + 1)
            dve.tensor_tensor(resid[:, p, :], PS[:, 7, 0:D], zbo[:, p, :], ALU.add).then_inc(res_ready, 1)
            dve.wait_ge(res_ready, n + 1)
            dve.bn_stats(st1[:, 1, p, :], resid[:, p, :]).then_inc(r_bn, 1)
            wait_apart(dve, r_bn, n + 1, waited_dve)
            dve.bn_aggr(mv1[:, 1, p, :], st1[:, 1, p, :]).then_inc(r_stats, 1)
            dve.wait_ge(r_rstd, n + 1)
            dve.tensor_scalar(resid[:, p, :], resid[:, p, :], mv1[:, 1, p, 0:1], rs1[:, 1, p:p + 1],
                              ALU.subtract, ALU.mult).then_inc(r_own, 1)
            dve.wait_ge(r_own, 2 * n + 1)
            dve.tensor_tensor(resid[:, p, :], resid[:, p, :], lngb[:], ALU.mult).then_inc(r_own, 1)
            dve.wait_ge(r_own, 2 * n + 2)
            dve.tensor_tensor(X[:, n, :], X[:, n, :], resid[:, p, :], ALU.add).then_inc(x3_ready, 1)

        def body(b, n, p, first, last_tile):
            if not last_tile:
                norm(n + 1, 1 - p)
            normalize_probs(n, p)
            if not last_tile:
                probs(n + 1, 1 - p)
            if not first:
                logits(n - 1)
            dve.wait_ge(tp_done, n + 1)
            dve.tensor_copy(pcT[:, 8, :], PS[:, 6, 0:P]).then_inc(tp_dve, 1)
            r = HK - 9 * P
            dve.tensor_copy(pcT[0:r, 9, :], PS[0:r, 6, P:2 * P]).then_inc(tp_dve, 1)
            finish(n, p)

        norm(0, 0, True)
        probs(0, 0)
        pairs(dve, body)
        logits(NT - 1)

    def act_cross(act):
        def turned(n, p):
            act.wait_ge(c_zT, n + 1)
            act.activation(zcT[:, p, :], PS[:, 0, 0:D], ACT.Copy).then_inc(c_zT_ready, 1)

        def numerators(n, p):
            act.wait_ge(sc_read, n + 1)
            act.activation(pc[:, p, :], pc[:, p, :], ACT.Exp).then_inc(pexp_ready, 1)

        def body(b, n, p, first, last_tile):
            if not last_tile:
                turned(n + 1, 1 - p)
            if not first:
                copy_x3T(n - 1, 1 - p)
            act.wait_ge(tp_done, n + 1)
            for half in range(2):
                act.activation(pcT[:, 4 * half:4 * half + 4, :], PS[:, 4 + half, :].rearrange("p (c n) -> p c n", c=4),
                               ACT.Copy).then_inc(tp_act, 1)
            if not last_tile:
                numerators(n + 1, 1 - p)

        def copy_x3T(n, p):
            act.wait_ge(x3T_done, n + 1)
            act.activation(x3T[:, p, :], PS[:, 7, D:2 * D], ACT.Copy).then_inc(x3T_ready, 1)
        turned(0, 0)
        numerators(0, 0)
        pairs(act, body)
        copy_x3T(NT - 1, 1)

    def pool_cross(pool):
        def root(n, i, p, stats, var, done):
            wait_apart(pool, stats, n + 1, waited_pool)
            pool.tensor_scalar(rs1[:, i, p:p + 1], mv1[:, i, p, 1:2], LN_EPS, None, ALU.add).then_inc(var, 1)
            pool.wait_ge(var, n + 1)
            pool.tensor_tensor(rs1[:, i, p:p + 1], rs1[:, i, p:p + 1], minus_half[:, 0:1], ALU.pow).then_inc(done, 1)

        def after_norm(n, p):
            root(n, 0, p, c_stats, c_var, c_rstd)
            pool.wait_ge(c_z, n + 1)
            pool.tensor_tensor(zbo[:, p, :], zc[:, p, :], bob[:], ALU.add).then_inc(c_zb, 1)
            pool.tensor_tensor(X[:, n, :], X[:, n, :], lnbb[:], ALU.add).then_inc(x_beta, 1)

        def body(b, n, p, first, last_tile):
            if not last_tile:
                after_norm(n + 1, 1 - p)
            root(n, 1, p, r_stats, r_var, r_rstd)
            wait_apart(pool, x3_ready, n + 1, waited_pool)
            pool.tensor_copy(x3[:, p, :], X[:, n, :]).then_inc(x3_copied, 1)
        pool.wait_ge(cross_in, 16 * CROSS_LOADS)
        pool.wait_ge(tanh_ready, 1)
        pool.tensor_scalar(lngb[:], lngb[:], tg[:, 1:2], None, ALU.mult).then_inc(lnb_scaled, 1)
        pool.tensor_scalar(lnbb[:], lnbb[:], tg[:, 1:2], None, ALU.mult).then_inc(lnb_scaled, 1)
        pool.wait_ge(lnb_scaled, 2)
        after_norm(0, 0)
        pairs(pool, body)

    CROSS_LOADS = 5

    def sp_cross(sp):
        sp.wait_ge(fold_read, FOLD_ALL)
        sp.dma_start(bob[:], t["L1_xattn_bo"].partition_broadcast(P)).then_inc(cross_in, 16)
        sp.dma_start(lngb[:], t["L1_xattn_ln_gamma"].partition_broadcast(P)).then_inc(cross_in, 16)
        sp.dma_start(lnbb[:], t["L1_xattn_ln_beta"].partition_broadcast(P)).then_inc(cross_in, 16)
        sp.dma_start(wr[:], t["L1_ffn_Wr"].rearrange("(k p) n -> p k n", p=P)).then_inc(cross_in, 16)
        sp.dma_start(brb[:], t["L1_ffn_br"].partition_broadcast(P)).then_inc(cross_in, 16)

    def pool_consts(pool):
        pool.memset(fill[:], NO_TOKEN).then_inc(const_set, 1)
        pool.memset(upper[:], 1.0).then_inc(const_set, 1)
        pool.memset(onesq[:], 1.0).then_inc(const_set, 1)
        pool.iota(iotas[:, 0, 0:E], pattern=[[1, E]], base=0, channel_multiplier=0,
                  allow_small_or_imprecise_dtypes=True).then_inc(const_set, 1)
        pool.iota(iotas[:, 1, 0:SLOTS], pattern=[[1, SLOTS]], base=0, channel_multiplier=0,
                  allow_small_or_imprecise_dtypes=True).then_inc(const_set, 1)
        pool.iota(iotas[:, 2, 0:NT], pattern=[[P, NT]], base=0, channel_multiplier=1,
                  allow_small_or_imprecise_dtypes=True).then_inc(const_set, 1)
        pool.wait_ge(const_set, 6)
        pool.affine_select(out=upper[:], in_=upper[:], compare_op=ALU.is_gt, fill=0.0, base=0,
                           pattern=[[1, P]], channel_multiplier=-1).then_inc(const_set, 1)

    def pool_fill(pool):
        rows = t["sorted"].rearrange("(n p) r -> p n r", p=P)
        for p, (n0, n1) in enumerate(((0, SLOTS // 2), (SLOTS // 2, SLOTS))):
            pool.dma_start(rows[:, n0:n1, :], fill[:].unsqueeze(1).to_broadcast([P, n1 - n0, ROW]))                 .then_inc(out_rows[p], 16)

    flat = lambda v: v.rearrange("p t e -> p (t e)")

    def pe_route(pe):
        pe.wait_ge(x3T_ready, NT)
        pe.wait_ge(sc_read, NT)
        pe.wait_ge(const_set, 7)
        for k in range(KC):
            last = pe.matmul(PS[:, 2, 0:E], onesq[:], wr[:, k, :], start=k == 0, stop=k == KC - 1)
        last.then_inc(wr_summed, 1)
        pe.wait_ge(oh_ready, 1)
        pe.matmul(PS[:, 0, 0:NT * E], upper[:], flat(RT[:, 1]), start=True, stop=True)
        pe.matmul(PS[:, 1, 0:NT * E], onesq[:], flat(RT[:, 1]), start=True, stop=True).then_inc(rank_done, 1)

    def act_route(act):
        act.wait_ge(gexp_in, 1)
        act.activation(RT[:, 0], RT[:, 0], ACT.Exp).then_inc(gexp_ready, 1)

    def dve_route(dve):
        own = Count(dve, route_own)
        onehot, rank, total, ca, cb, slots_of = RT[:, 1], RT[:, 2], RT[:, 3], RT[:, 4], RT[:, 5], RT[:, 6]
        small = lambda k: RT[:, 7 + k // NT, k % NT, :]
        bc_t = lambda v: v.unsqueeze(1).to_broadcast([P, NT, E])
        bc_e = lambda v: v.unsqueeze(2).to_broadcast([P, NT, E])
        dve.wait_ge(const_set, 7)
        dve.wait_ge(lg_ready, NT)
        dve.wait_ge(x3_stats, NT)
        for n in range(NT):
            last = dve.bn_aggr(meanvar[:, n, :], stats[:, n, :])
        last.then_inc(x3_meanvar, 1)
        dve.wait_ge(wr_summed, 1)
        own.add(dve.tensor_copy(small(0), PS[:, 2, 0:E]))
        own.wait()
        dve.wait_ge(x3_meanvar, 1)
        own.add(dve.tensor_tensor(RT[:, 0], bc_t(small(0)), bc_e(meanvar[:, 0:NT, 0]), ALU.mult))
        own.wait()
        own.add(dve.tensor_tensor(LG[:], LG[:], RT[:, 0], ALU.subtract))
        own.add(dve.tensor_copy(XR[:, :, MEAN], meanvar[:, 0:NT, 0]))
        own.add(dve.tensor_copy(XR[:, :, TOKEN], iotas[:, 2, 0:NT]))
        own.wait()
        dve.wait_ge(x3_once, 1)
        own.add(dve.tensor_tensor(LG[:], LG[:], bc_e(rs[:, 0, 0:NT]), ALU.mult))
        own.wait()
        own.add(dve.tensor_tensor(LG[:], LG[:], bc_t(brb[:]), ALU.add))
        own.wait()
        for n in range(NT):
            last = dve.max(out=top[:, n, :], in_=LG[:, n, :])
        own.add(last)
        own.wait()
        for n in range(NT):
            last = dve.max_index(out=topi[:, n, :], in_max=top[:, n, :], in_values=LG[:, n, :])
        own.add(last)
        dve.tensor_tensor(RT[:, 0], LG[:], bc_e(top[:, :, 0]), ALU.subtract).then_inc(gexp_in, 1)
        own.wait()
        own.add(dve.tensor_copy(rtn[:, 0, :], topi[:, :, 0]))
        own.wait()
        dve.tensor_tensor(onehot, bc_t(iotas[:, 0, 0:E]), bc_e(rtn[:, 0, :]), ALU.is_equal).then_inc(oh_ready, 1)
        dve.wait_ge(gexp_ready, 1)
        own.add(dve.tensor_reduce(rtn[:, 1, :], RT[:, 0], AX.X, ALU.add))
        own.wait()
        own.add(dve.reciprocal(rtn[:, 1, :], rtn[:, 1, :]))
        own.wait()
        own.add(dve.tensor_scalar(XR[:, :, GATE], rtn[:, 1, :], tg[:, 3:4], None, ALU.mult))
        dve.wait_ge(rank_done, 1)
        own.add(dve.tensor_copy(flat(rank), PS[:, 0, 0:NT * E]))
        own.add(dve.tensor_copy(flat(total), PS[:, 1, 0:NT * E]))
        own.wait()
        src, dst, step = total, ca, 1
        while step < NT:
            own.add(dve.tensor_copy(dst[:, 0:step, :], src[:, 0:step, :]))
            own.add(dve.tensor_tensor(dst[:, step:, :], src[:, step:, :], src[:, 0:NT - step, :], ALU.add))
            own.wait()
            src, dst, step = dst, (cb if dst is ca else ca), 2 * step
        counts = src[:, NT - 1, :]
        own.add(dve.tensor_scalar(small(0), counts, float(P - 1), None, ALU.add))
        own.wait()
        own.add(dve.tensor_copy(rti[:, 0:E], small(0)))
        own.wait()
        own.add(dve.tensor_scalar(rti[:, 0:E], rti[:, 0:E], P.bit_length() - 1, None, ALU.arith_shift_right))
        own.wait()
        own.add(dve.tensor_copy(small(1), rti[:, 0:E]))
        own.wait()
        tiles, at, step = small(1), 2, 1
        total_tiles = tiles
        while step < E:
            nxt = small(at)
            own.add(dve.tensor_copy(nxt[:, 0:step], total_tiles[:, 0:step]))
            own.add(dve.tensor_tensor(nxt[:, step:], total_tiles[:, step:], total_tiles[:, 0:E - step], ALU.add))
            own.wait()
            total_tiles, at, step = nxt, at + 1, 2 * step
        first_row = small(at)
        own.add(dve.tensor_tensor(first_row, total_tiles, tiles, ALU.subtract))
        own.add(dve.tensor_tensor(slots_of, src, total, ALU.subtract))
        own.wait()
        own.add(dve.tensor_scalar(first_row, first_row, float(P), None, ALU.mult))
        own.add(dve.tensor_tensor(slots_of, slots_of, rank, ALU.add))
        own.wait()
        own.add(dve.tensor_tensor(slots_of, slots_of, bc_t(first_row), ALU.add))
        own.wait()
        own.add(dve.tensor_tensor(slots_of, slots_of, onehot, ALU.mult))
        own.wait()
        own.add(dve.tensor_reduce(rtn[:, 2, :], slots_of, AX.X, ALU.add))
        own.wait()
        own.add(dve.tensor_copy(slot[:], rtn[:, 2, :]))
        own.wait()
        dve.engine_nop().then_inc(slot_ready, 1)
        ends = RT[:, 0:2].rearrange("p a t e -> p (a t) e")[:, 0:SLOTS, :]
        own.add(dve.tensor_tensor(ends, total_tiles.unsqueeze(1).to_broadcast([P, SLOTS, E]),
                                  iotas[:, 1, 0:SLOTS].unsqueeze(2).to_broadcast([P, SLOTS, E]), ALU.is_le))
        own.wait()
        own.add(dve.tensor_reduce(top[:, 0:4, :].rearrange("p a b -> p (a b)")[:, 0:SLOTS], ends, AX.X, ALU.add))
        own.wait()
        dve.tensor_scalar(expert_of[:], top[:, 0:4, :].rearrange("p a b -> p (a b)")[:, 0:SLOTS], float(E - 1), None,
                          ALU.min).then_inc(expert_ready, 1)

    def pool_route(pool):
        pool.wait_ge(x3_meanvar, 1)
        own = Count(pool, pool_own, 6)
        var, once, twice = meanvar[:, 0:NT, 1], rs[:, 0, 0:NT], rs[:, 1, 0:NT]
        root = minus_half[:, 0:NT]
        own.add(pool.tensor_scalar(once, var, LN_EPS, None, ALU.add))
        own.wait()
        own.add(pool.tensor_tensor(once, once, root, ALU.pow))
        own.wait()
        pool.engine_nop().then_inc(x3_once, 1)
        for ins in (lambda: pool.tensor_tensor(twice, var, once, ALU.mult),
                    lambda: pool.tensor_tensor(twice, twice, once, ALU.mult),
                    lambda: pool.tensor_scalar(twice, twice, LN_EPS, None, ALU.add),
                    lambda: pool.tensor_tensor(twice, twice, root, ALU.pow),
                    lambda: pool.tensor_tensor(XR[:, :, ROOT], twice, once, ALU.mult)):
            own.add(ins())
            own.wait()
        pool.wait_ge(slot_ready, 1)
        for p in range(2):
            pool.wait_ge(out_rows[p], 16)
        for n in range(NT):
            pool.indirect_dma_start(t["sorted"], bass.IndirectOffsetOnAxis(ap=slot[:, n:n + 1], axis=0),
                                    XR[:, n, :], None).then_inc(scattered, 16)

    def sp_experts_loads(sp):
        sp.wait_ge(lif_done, 2 * NG + 2)
        for e in range(E):
            sp.dma_start(w1[:, e, :, :], t["L1_ffn_W1"][e].rearrange("(k p) f -> p k f", p=P)).then_inc(w1_in[0], 16)
        sp.wait_ge(pvc_done, NT)
        for e in range(E):
            sp.dma_start(w2[:, e, :, :], t["L1_ffn_W2"][e].rearrange("(c p) d -> p c d", p=P)).then_inc(w2_in[0], 16)
        sp.wait_ge(oh_ready, 1)
        sp.dma_start(b2[:], t["L1_ffn_b2"].rearrange("(a e) d -> a (e d)", a=1)).then_inc(b2_in, 16)

    def slot_tiles(eng, body):
        rounds = (SLOTS - 2) // 4
        with eng.Fori(0, rounds) as i:
            for u in range(4):
                body(4 * i + u, u, True, True)
        for n in range(4 * rounds, SLOTS):
            body(n, n % 4, n + 1 < SLOTS, n + 2 < SLOTS)

    def sp_experts(sp):
        def load(n, u, nxt, after):
            sp.wait_ge(oe_ready, n + 1)
            sp.dma_start(xe[:, u, :], t["sorted"][ds(n * P, P), :]).then_inc(xe_in[u], 16)
        sp.wait_ge(scattered, 16 * NT)
        slot_tiles(sp, load)

    of_buffer = lambda n, u: 4 * n + (16 - 4 * u)
    of_parity = lambda n, p: 8 * n + (16 - 8 * p)

    def dve_experts(dve):
        def norm(n, u):
            p = u % 2
            dve.wait_ge(xe_in[u], of_buffer(n, u))
            dve.tensor_scalar(ze[:, p, :], xe[:, u, 0:D], xe[:, u, MEAN:MEAN + 1], xe[:, u, ROOT:ROOT + 1],
                              ALU.subtract, ALU.mult).then_inc(e_z, 1)

        def hidden(n, p):
            dve.wait_ge(g1_done, n + 1)
            dve.tensor_copy(he[:, p, 512:F], PS[:, 2 + 4 * p + p, :]).then_inc(he_dve, 1)

        def activate(n, p):
            e = dve.value_load(expert_of[0:1, ds(n, 1)], min_val=0, max_val=E - 1)
            dve.wait_ge(heT_done, n + 1)
            for c in range(4, FC):
                last = dve.tensor_scalar(heT[:, c, :], PS[:, 4, (c - 4) * P:(c - 3) * P], b1f[:, ds(e * FC + c, 1)], 0.0,
                                         ALU.add, ALU.max)
            last.then_inc(heT_dve, 1)

        def finish(n, u):
            p = u % 2
            dve.wait_ge(out_rows[p], of_parity(n, p))
            dve.tensor_copy(token[:, p:p + 1], xe[:, u, TOKEN:TOKEN + 1]).then_inc(e_token, 1)
            dve.wait_ge(g2_done, n + 1)
            dve.scalar_tensor_tensor(oe[:, p, :], PS[:, 5, 0:D], xe[:, u, GATE:GATE + 1], xe[:, u, 0:D],
                                     ALU.mult, ALU.add).then_inc(oe_ready, 1)

        def body(n, u, nxt, after):
            if after:
                norm(n + 2, (u + 2) % 4)
            if nxt:
                hidden(n + 1, 1 - u % 2)
            activate(n, u % 2)
            finish(n, u)
        dve.wait_ge(expert_ready, 1)
        norm(0, 0)
        norm(1, 1)
        hidden(0, 0)
        slot_tiles(dve, body)

    b1f = b1[:].rearrange("p e c -> p (e c)")

    def act_experts(act):
        def affine(n, p):
            act.wait_ge(e_zT, n + 1)
            for k in range(KC):
                last = act.activation(xeT[:, p, k, :], PS[:, 0, k * P:k * P + P], ACT.Identity,
                                      bias=leb[:, k:k + 1], scale=leg[:, k:k + 1])
            last.then_inc(e_zT_ready, 1)

        def hidden(n, p):
            act.wait_ge(g1_done, n + 1)
            act.activation(he[:, p, 0:512], PS[:, 1 + 4 * p + p, :], ACT.Copy).then_inc(he_act, 1)

        def activate(n, p):
            e = act.value_load(expert_of[0:1, ds(n, 1)], min_val=0, max_val=E - 1)
            act.wait_ge(heT_done, n + 1)
            for c in range(4):
                last = act.activation(heT[:, c, :], PS[:, 3, c * P:c * P + P], ACT.Relu, bias=b1f[:, ds(e * FC + c, 1)])
            last.then_inc(heT_act, 1)

        def body(n, u, nxt, after):
            p = u % 2
            if nxt:
                hidden(n + 1, 1 - p)
            activate(n, p)
            if after:
                affine(n + 2, p)
        act.wait_ge(expert_ready, 1)
        affine(0, 0)
        hidden(0, 0)
        affine(1, 1)
        slot_tiles(act, body)

    def pe_experts(pe):
        def turn(n, p):
            pe.wait_ge(e_z, n + 1)
            for k in range(KC):
                last = pe.transpose(PS[:, 0, k * P:k * P + P], ze[:, p, k * P:k * P + P], ident[:])
            last.then_inc(e_zT, 1)

        def up(n, p):
            e = pe.value_load(expert_of[0:1, ds(n, 1)], min_val=0, max_val=E - 1)
            pe.wait_ge(e_zT_ready, n + 1)
            w = w1[:].rearrange("p e k f -> p (e k f)")
            for half in range(2):
                for k in range(KC):
                    last = pe.matmul(PS[:, 1 + half + 5 * p, :], xeT[:, p, k, :], w[:, ds(e * (KC * F) + k * F + half * 512, 512)],
                                     start=k == 0, stop=k == KC - 1)
            last.then_inc(g1_done, 1)

        def turn_hidden(n, p):
            pe.wait_ge(he_act, n + 1)
            pe.wait_ge(he_dve, n + 1)
            for c in range(FC):
                last = pe.transpose(PS[:, 3 + c // 4, c % 4 * P:c % 4 * P + P], he[:, p, c * P:c * P + P], ident[:])
            last.then_inc(heT_done, 1)

        def down(n, p):
            e = pe.value_load(expert_of[0:1, ds(n, 1)], min_val=0, max_val=E - 1)
            pe.wait_ge(oe_ready, n + 4)
            pe.wait_ge(heT_act, n + 1)
            pe.wait_ge(heT_dve, n + 1)
            w = w2[:].rearrange("p e c d -> p (e c d)")
            for c in range(FC):
                pe.matmul(PS[:, 5, 0:D], heT[:, c, :], w[:, ds(e * (FC * D) + c * D, D)], start=c == 0, stop=False)
            pe.matmul(PS[:, 5, 0:D], ones[:], b2[:, ds(e * D, D)], start=False, stop=True).then_inc(g2_done, 1)

        def body(n, u, nxt, after):
            p = u % 2
            if nxt:
                up(n + 1, 1 - p)
            turn_hidden(n, p)
            if after:
                turn(n + 2, p)
            down(n, p)
        pe.wait_ge(expert_ready, 1)
        pe.wait_ge(w1_in[0], 16 * E)
        turn(0, 0)
        up(0, 0)
        turn(1, 1)
        pe.wait_ge(w2_in[0], 16 * E)
        pe.wait_ge(b2_in, 16)
        pe.wait_ge(ones1_set, 1)
        slot_tiles(pe, body)

    def pool_experts(pool):
        def send(n, p):
            pool.wait_ge(oe_ready, n + 5)
            wait_apart(pool, e_token, n + 1, waited_pool)
            pool.indirect_dma_start(t["out"].rearrange("b s d -> (b s) d"),
                                    bass.IndirectOffsetOnAxis(ap=token[:, p:p + 1], axis=0), oe[:, p, :], None,
                                    bounds_check=B * S - 1, oob_is_err=False).then_inc(out_rows[p], 16)

        def body(n, u, nxt, after):
            send(n, u % 2)
        slot_tiles(pool, body)
        for p in range(2):
            pool.wait_ge(out_rows[p], 16 + 16 * ((SLOTS + 1 - p) // 2))

    block = ctx.enter_context(nc.Block())

    @block.sync
    def _(sp):
        xv = t["x"].rearrange("b (t p) d -> p (b t) d", p=P)
        for g in range(NG):
            sp.dma_start(X[:, GT * g:GT * g + GT, :], xv[:, GT * g:GT * g + GT, :]).then_inc(x_in[g], 16)
        sp.wait_ge(zero_set, 1)
        sp.dma_start(ctxn[0:C, :, :], t["ctx_1024"].rearrange("b c d -> c b d")).then_inc(ctx_in, 16)
        sp.dma_start(wqkv[:, :, 0:D], t["L0_xattn_W_q"].rearrange("(k p) n -> p k n", p=P)).then_inc(wts_in, 16)
        sp.dma_start(wqkv[:, :, D:3 * D], t["L0_xattn_W_kv"].rearrange("(k p) n -> p k n", p=P)).then_inc(wts_in, 16)
        sp.dma_start(wout[:], t["L0_xattn_W_out"].rearrange("(h e) n -> e h n", e=E0)).then_inc(wts_in, 16)
        for w, name in ((wk1, "L1_xattn_Wk"), (wv1, "L1_xattn_Wv"), (wq1, "L1_xattn_Wq")):
            sp.dma_start(w[:], t[name].rearrange("(k p) n -> p k n", p=P)).then_inc(fold_in, 16)
        sp.dma_start(wo1[:], t["L1_xattn_Wo"].rearrange("(c p) n -> p c n", p=P)).then_inc(fold_in, 16)
        sp_fold(sp)
        sp_cross(sp)
        sp_experts_loads(sp)
        sp_experts(sp)

    @block.gpsimd
    def _(pool):
        pool.memset(ctxn[:], 0.0).then_inc(zero_set, 1)
        pool.memset(ident[:], 0.0).then_inc(ident_set, 1)
        pool.memset(minus_half[:], -0.5).then_inc(half_set, 1)
        pool.wait_ge(ident_set, 1)
        pool.affine_select(out=ident[:], in_=ident[:], compare_op=ALU.not_equal, fill=1.0, base=0,
                           pattern=[[-1, P]], channel_multiplier=1).then_inc(ident_set, 1)
        pool_norm(pool)
        pool_consts(pool)
        pool.wait_ge(wts_in, 48)
        pool.wait_ge(tanh_ready, 1)
        pool.tensor_scalar(wout[:], wout[:], tg[0:E0, 0:1], None, ALU.mult).then_inc(wout_scaled, 1)
        pool.tensor_scalar(boutb[:], boutb[:], tg[:, 0:1], None, ALU.mult).then_inc(wout_scaled, 1)
        pool.tensor_scalar(tg5[:], tg[:, 2:3], 0.2, None, ALU.mult).then_inc(tg_ready, 1)
        pool.wait_ge(wout_scaled, 2)
        with pool.Fori(0, B) as b:
            pool_project(pool, b)
        pool.wait_ge(proj_added, 2 * MP * B)
        pool.memset(bqz[:], 0.0).then_inc(zeroed, 1)
        pool_fill(pool)
        pool_ffn(pool)
        pool_cross(pool)
        pool_route(pool)
        pool_experts(pool)

    @block.scalar
    def _(act):
        def column(dst, name, k):
            act.dma_start(dst, t[name].rearrange("(k p) -> p k", k=k),
                          allow_slow_non_contiguous=True).then_inc(vec_in, 16)
        act.dma_start(gates[:, 0:2], t["g_xattn"].partition_broadcast(P)).then_inc(vec_in, 16)
        act.dma_start(gates[:, 2:4], t["g_ffn"].partition_broadcast(P)).then_inc(vec_in, 16)
        act.dma_start(boutb[:], t["L0_xattn_b_out"].partition_broadcast(P)).then_inc(vec_in, 16)
        column(lnlg[:], "L0_xattn_ln_l_g", KC)
        column(lnlb[:], "L0_xattn_ln_l_b", KC)
        column(lnxg[:], "L0_xattn_ln_x_g", KC)
        column(lnxb[:], "L0_xattn_ln_x_b", KC)
        for lo in (0, E0):
            column(qgam[lo:lo + E0, :], "L0_xattn_q_gamma", 1)
            column(kgam[lo:lo + E0, :], "L0_xattn_k_gamma", 1)
        act.dma_start(masku[:], t["mask_BxS2_bk0"].rearrange("(a b) c -> a b c", a=1)).then_inc(vec_in, 16)
        column(bk1[:], "L1_xattn_bk", FC)
        column(bv1[:], "L1_xattn_bv", FC)
        column(leg[:], "L1_ffn_ln_g", KC)
        column(leb[:], "L1_ffn_ln_b", KC)
        act.dma_start(b1[:], t["L1_ffn_b1"].rearrange("e (c p) -> p e c", p=P),
                      allow_slow_non_contiguous=True).then_inc(vec_in, 16)
        act.wait_ge(vec_in, 16 * VECS)
        act.activation(tg[:], gates[:], ACT.Tanh).then_inc(tanh_ready, 1)
        act.wait_ge(gam_scaled, 1)
        with act.Fori(0, B) as b:
            act_project(act, b)
            act_attend(act, b)
        act_ffn(act)
        act_cross(act)
        act_route(act)
        act_experts(act)

    @block.tensor
    def _(pe):
        pe.wait_ge(ident_set, 2)
        pe.wait_ge(wts_in, 48)
        pe.wait_ge(mask_set, 3)
        with pe.Fori(0, B) as b:
            pe_project(pe, b)
            pe_attend(pe, b)
        pe_fold(pe)
        pe_ffn(pe)
        pe.wait_ge(ones_set, 3)
        pe_cross(pe)
        pe_route(pe)
        pe_experts(pe)

    @block.vector
    def _(dve):
        dve_norm(dve)
        dve.wait_ge(vec_in, 16 * VECS)
        dve.tensor_scalar(qgam[:], qgam[:], E0 ** -0.5, None, ALU.mult).then_inc(gam_scaled, 1)
        dve.memset(onesr[:].bitcast(F32), 1.0).then_inc(mask_set, 1)
        dve.memset(maskr[:].bitcast(F32), 0.0).then_inc(mask_set, 1)
        dve.wait_ge(mask_set, 2)
        dve.tensor_scalar(maskr[:, :, 0:C], masku[:], 1.0, MASKED, ALU.subtract, ALU.mult).then_inc(mask_set, 1)
        dve.memset(ones33[:].bitcast(F32), 0.0).then_inc(ones_set, 1)
        dve.wait_ge(ones_set, 1)
        dve.memset(ones33[0:1, :].bitcast(F32), 1.0).then_inc(ones_set, 1)
        dve.memset(ones33[32:33, :].bitcast(F32), 1.0).then_inc(ones_set, 1)
        dve.memset(spikes[:, 0:1], 0.0).then_inc(lif_done, 2)
        dve.memset(spikes[:, 1:2], 0.0).then_inc(y_done, 1)
        dve.memset(spikes[:, 2:3], 0.0).then_inc(oe_ready, 4)
        dve.wait_ge(rstd_ready, 2)
        with dve.Fori(0, B) as b:
            dve_project(dve, b)
            dve_attend(dve, b)
        dve_fold(dve)
        dve.wait_ge(tg_ready, 1)
        dve_ffn(dve)
        dve_cross(dve)
        dve_route(dve)
        dve.memset(ones[:], 1.0).then_inc(ones1_set, 1)
        dve_experts(dve)
    ctx.close()


def build(nc, shapes):
    t = {}
    for name, (shape, dt) in shapes.items():
        t[name] = nc.dram_tensor(f"in_{name}", list(shape), dt, kind="ExternalInput").ap()
    t["out"] = nc.dram_tensor("out", [B, S, D], F32, kind="ExternalOutput").ap()
    t["vw_rows"] = nc.dram_tensor("vw_rows", [B, HK, D], F32).ap()
    t["sorted"] = nc.dram_tensor("sorted", [SLOTS * P, ROW], F32).ap()
    layers_kernel(nc, t)


def kernel(**inputs):
    import concourse.bacc as bacc
    from concourse.bass_utils import run_bass_kernel_spmd

    nc = bacc.Bacc("TRN2", target_bir_lowering=False, num_devices=1)
    arrays, shapes = {}, {}
    for name, a in inputs.items():
        a = np.ascontiguousarray(a)
        arrays[f"in_{name}"] = a
        shapes[name] = (a.shape, mybir.dt.from_np(a.dtype))
    build(nc, shapes)
    r = run_bass_kernel_spmd(nc, [arrays], core_ids=[0])
    return r.results[0]["out"]
```

```python
from contextlib import ExitStack

import numpy as np
import concourse.bass as bass
from concourse import mybir

F32 = mybir.dt.float32
F32R = mybir.dt.float32r
U8 = mybir.dt.uint8
U32 = mybir.dt.uint32
I32 = mybir.dt.int32
ALU = mybir.AluOpType
ACT = mybir.ActivationFunctionType
AX = mybir.AxisListType
ds = bass.ds

P = 128
B, S, D = 2, 1024, 256
KC = D // P
NT = B * S // P
GT = 4
GN = GT * P
NG = NT // GT
BG = NG // B
C = 77
H0, E0 = 4, 64
KEYS = S + C
KPAD = KEYS + 1
KT = S // P + 1
F = 1024
FC = F // P
H1 = 16
HK = H1 * C
HC = -(-HK // P)
E = 8
ROW = D + 4
GATE, TOKEN, MEAN, ROOT = D, D + 1, D + 2, D + 3
SLOTS = (B * S - E) // P + E
NO_TOKEN = 4096.0
LN_EPS = 1e-5
RMS_EPS = 1e-8
MASKED = 1e30


def spike_edges(steps=5, beta=0.9, threshold=1.0):
    f = np.float32

    def spikes(y):
        mem, count = f(0), 0
        for _ in range(steps):
            mem = f(f(f(beta) * mem) + y) - f(mem > threshold)
            count += int(mem > threshold)
        return count
    edges = []
    for n in range(1, steps + 1):
        lo, hi = f(0), f(4)
        while np.nextafter(lo, hi) < hi:
            mid = f((lo + hi) / 2)
            lo, hi = (mid, hi) if spikes(mid) < n else (lo, mid)
        edges.append(float(lo))
    return edges


class Ring:

    def __init__(self, eng, full, free, banks):
        self.eng, self.full, self.free, self.banks, self.n = eng, full, free, banks, 0

    def to_fill(self):
        if self.n >= len(self.banks):
            self.eng.wait_ge(self.free, self.n - len(self.banks) + 1)
        return self.banks[self.n % len(self.banks)]

    def filled(self, ins):
        ins.then_inc(self.full, 1)
        self.n += 1

    def to_read(self):
        self.eng.wait_ge(self.full, self.n + 1)
        return self.banks[self.n % len(self.banks)]

    def read(self, ins):
        ins.then_inc(self.free, 1)
        self.n += 1


class Count:

    def __init__(self, eng, sem, base=0):
        self.eng, self.sem, self.base, self.n = eng, sem, base, 0

    def add(self, ins):
        self.n += 1
        return ins.then_inc(self.sem, 1)

    def wait(self):
        self.eng.wait_ge(self.sem, self.base + self.n)


def wait_apart(eng, sem, value, waited):
    eng.wait_ge(sem, value)
    eng.sem_inc(waited, 1)


def layers_kernel(nc, t):
    ctx = ExitStack()
    floats = {}

    def sb(where, name, shape, dt=F32):
        floats[id(where)] = floats.get(id(where), 0) + 8 * -(-int(np.prod(shape[1:])) // 8)
        return where.enter_context(nc.sbuf_tensor(name, shape, dt))
    sem = lambda name: ctx.enter_context(nc.semaphore(name))

    PS = ctx.enter_context(nc.psum_tensor("PS", [P, 8, 512], F32))
    PSf = PS[:].rearrange("p k n -> p (k n)")

    XR = sb(ctx, "XR", [P, NT, ROW])
    X = XR[:, :, 0:D]
    ident = sb(ctx, "ident", [P, P])
    ones33 = sb(ctx, "ones33", [33, P], F32R)
    gates = sb(ctx, "gates", [P, 4])
    tg = sb(ctx, "tg", [P, 4])
    tg5 = sb(ctx, "tg5", [P, 1])
    minus_half = sb(ctx, "minus_half", [P, 32])
    ctxn = sb(ctx, "ctxn", [P, B, D])
    stats = sb(ctx, "stats", [P, NT + B, 6])
    meanvar = sb(ctx, "meanvar", [P, NT + B, 2])
    rs = sb(ctx, "rs", [P, 3, NT + B])
    rstd = sb(ctx, "rstd", [P, NT + B])
    Z = sb(ctx, "Z", [P, GT, D])

    stg = sb(ctx, "stg", [P, GT, 6])
    mvg = sb(ctx, "mvg", [P, GT, 2])
    rsg = sb(ctx, "rsg", [P, GT])
    bq1 = sb(ctx, "bq1", [P, FC])
    bk1 = sb(ctx, "bk1", [P, FC])
    bv1 = sb(ctx, "bv1", [P, FC])
    LG = sb(ctx, "LG", [P, NT, E])
    fill = sb(ctx, "fill", [P, ROW])
    upper = sb(ctx, "upper", [P, P])
    onesq = sb(ctx, "onesq", [P, P])
    iotas = sb(ctx, "iotas", [P, 3, SLOTS])
    slot = sb(ctx, "slot", [P, NT], U32)
    expert_of = sb(ctx, "expert_of", [P, SLOTS], I32)
    leg = sb(ctx, "leg", [P, KC])
    leb = sb(ctx, "leb", [P, KC])
    b1 = sb(ctx, "b1", [P, E, FC])

    att = ExitStack()
    QS = sb(att, "QS", [P, BG, H0, GN], F32R)
    KH = sb(att, "KH", [P, H0, KPAD], F32R)
    KL = sb(att, "KL", [P, H0, KPAD], F32R)
    VHL = sb(att, "VHL", [P, KT, H0, 2, E0], F32R)
    prob = sb(att, "prob", [P, 2, GT, KEYS])
    OT = sb(att, "OT", [P, 2, GN])
    wqkv = sb(att, "wqkv", [P, KC, 3 * D])
    wout = sb(att, "wout", [P, H0, D])
    boutb = sb(att, "boutb", [P, D])
    lnlg = sb(att, "lnlg", [P, KC])
    lnlb = sb(att, "lnlb", [P, KC])
    lnxg = sb(att, "lnxg", [P, KC])
    lnxb = sb(att, "lnxb", [P, KC])
    qgam = sb(att, "qgam", [P, 1])
    kgam = sb(att, "kgam", [P, 1])
    masku = sb(att, "masku", [1, B, C], U8)
    maskr = sb(att, "maskr", [1, B, C + 1], F32R)
    ssum = sb(att, "ssum", [P, 2, 2 * H0])
    rms2 = sb(att, "rms2", [P, 2, 2 * H0])
    rrms = sb(att, "rrms", [P, 2, 2 * H0])
    nmax = sb(att, "nmax", [P, 2, GT])
    lsum = sb(att, "lsum", [P, 2, GT])
    rl = sb(att, "rl", [P, 2, GT])
    proj_buffers = ExitStack()
    lnT = sb(proj_buffers, "lnT", [P, KC, GN])
    sq = sb(proj_buffers, "sq", [P, 2, 2 * D])
    qk2 = sb(proj_buffers, "qk2", [P, 2, 2 * H0, 2, E0])
    proj_buffers.close()
    att_buffers = ExitStack()
    PB = 4
    PH = sb(att_buffers, "PH", [P, PB, GN], F32R)
    PL = sb(att_buffers, "PL", [P, PB, GN], F32R)
    att_buffers.close()
    att.close()

    late = ExitStack()
    keysT = sb(late, "keysT", [P, FC, B, 2, C])
    vwn = sb(late, "vwn", [C, H1, D])
    Zf = Z[:].rearrange("p s d -> p (s d)")
    ctxT = Zf[:, 0:KC * B * C].rearrange("p (k b c) -> p k b c", k=KC, b=B)
    bqz = Zf[:, KC * B * C:KC * B * C + FC * 33].rearrange("p (c n) -> p c n", c=FC)
    wfcH = sb(late, "wfcH", [P, KC, F], F32R)
    wfcL = sb(late, "wfcL", [P, KC, F], F32R)
    wprojT = sb(late, "wprojT", [P, FC, D])
    hT = sb(late, "hT", [P, FC, GN])
    wfc = hT[:, 0:FC // 2, :].rearrange("p a (b d) -> p (a b) d", d=D)
    wproj = hT[:, FC // 2:FC, :].rearrange("p (k a) n -> p k (a n)", k=KC)
    kwH = sb(late, "kwH", [P, KC, B, HK], F32R)
    kwL = sb(late, "kwL", [P, KC, B, HK], F32R)
    kc = sb(late, "kc", [33, B, HK], F32R)
    vw = sb(late, "vw", [P, B, HC, D])
    fold_buffers = ExitStack()
    wqT = sb(fold_buffers, "wqT", [P, FC, D])
    valsT = sb(fold_buffers, "valsT", [P, FC, B, C])
    fold_buffers.close()
    ffn_buffers = ExitStack()
    zTH = sb(ffn_buffers, "zTH", [P, KC, GN], F32R)
    zTL = sb(ffn_buffers, "zTL", [P, KC, GN], F32R)
    relu = sb(ffn_buffers, "relu", [P, 2, GN])
    spikes = sb(ffn_buffers, "spikes", [P, GN])
    ffn_buffers.close()
    cross_buffers = ExitStack()
    pcT = sb(cross_buffers, "pcT", [P, HC, P])
    x3T = sb(cross_buffers, "x3T", [P, 2, D])
    cross_buffers.close()
    late.close()

    moe = ExitStack()
    w1 = sb(moe, "w1", [P, E, KC, F])
    w2 = sb(moe, "w2", [P, E, FC, D])
    moe.close()

    BELOW = max(floats[id(att)] + max(floats[id(proj_buffers)], floats[id(att_buffers)]), floats[id(late)] + max(floats[id(fold_buffers)], floats[id(ffn_buffers)]), floats[id(moe)])
    above = ExitStack()
    above.enter_context(nc.sbuf_tensor("below", [P, BELOW], F32))
    wk1 = sb(above, "wk1", [P, KC, F])
    wv1 = sb(above, "wv1", [P, KC, F])
    wq1 = sb(above, "wq1", [P, KC, F])
    wo1 = sb(above, "wo1", [P, FC, D])
    above.close()
    above = ExitStack()
    above.enter_context(nc.sbuf_tensor("below2", [P, BELOW], F32))
    zc = sb(above, "zc", [P, 2, D])
    zbo = sb(above, "zbo", [P, 2, D])
    zcH = sb(above, "zcH", [P, 2, D], F32R)
    zcL = sb(above, "zcL", [P, 2, D], F32R)
    pc = sb(above, "pc", [P, 2, HK])
    resid = sb(above, "resid", [P, 2, D])
    x3 = sb(above, "x3", [P, 2, D])
    bob = sb(above, "bob", [P, D])
    lngb = sb(above, "lngb", [P, D])
    lnbb = sb(above, "lnbb", [P, D])
    mx1 = sb(above, "mx1", [P, 2, H1])
    sum1 = sb(above, "sum1", [P, 2, H1])
    st1 = sb(above, "st1", [P, 2, 2, 6])
    mv1 = sb(above, "mv1", [P, 2, 2, 2])
    st3 = sb(above, "st3", [P, 2, 6])
    mv3 = sb(above, "mv3", [P, 2, 2])
    rs1 = sb(above, "rs1", [P, 2, 2])
    wr = sb(above, "wr", [P, KC, E])
    brb = sb(above, "brb", [P, E])
    above.close()
    above = ExitStack()
    above.enter_context(nc.sbuf_tensor("below3", [P, BELOW], F32))
    xe = sb(above, "xe", [P, 4, ROW])
    ze = sb(above, "ze", [P, 2, D])
    xeT = sb(above, "xeT", [P, 2, KC, P])
    he = sb(above, "he", [P, F])
    heT = sb(above, "heT", [P, FC, P])
    oe = sb(above, "oe", [P, 2, D])
    token = sb(above, "token", [P, 2], U32)
    b2 = sb(above, "b2", [P, E * D])
    top = sb(above, "top", [P, 4, 8])
    RT = sb(above, "RT", [P, 10, NT, E])
    rti = sb(above, "rti", [P, E], I32)
    rtn = sb(above, "rtn", [P, 4, NT])
    above.close()

    sems = lambda names: [sem(name) for name in names.split()]
    (ctx_in, wts_in, vec_in, l1_in, moe_in, fold_in, vwo_done, vwo_read, ffn_in, vw_in, cross_in, w1_in, w2_in,
     b2_in, scattered) = sems(
         "ctx_in wts_in vec_in l1_in moe_in fold_in vwo_done vwo_read ffn_in vw_in cross_in w1_in w2_in b2_in "
         "scattered")
    (ident_set, zero_set, half_set, mask_set, ones_set, const_set, tanh_ready, gam_scaled,
     wout_scaled, tg_ready, lnb_scaled, waited_pool, waited_dve, dve_own, route_own) = sems(
         "ident_set zero_set half_set mask_set ones_set const_set tanh_ready gam_scaled "
         "wout_scaled tg_ready lnb_scaled waited_pool waited_dve dve_own route_own")
    (g_zT_low, fold_own, stats_ready, rstd_ready, pool_own, root_in, root_out, z_ready, zT_done, lnT_ready, qkv_done, v_done, v_high, v_low, sq_ready,
     ssum_ready, rms_mean, rrms_ready, qk2_ready, qkT_done, high_ready, low_ready, bias_added) = sems(
         "g_zT_low fold_own stats_ready rstd_ready pool_own root_in root_out z_ready zT_done lnT_ready qkv_done v_done v_high v_low sq_ready "
         "ssum_ready rms_mean rrms_ready qk2_ready qkT_done high_ready low_ready bias_added")
    (s_done, max_ready, exp_done, t_done, tile_high, tile_low, pv_done, ot_ready, proj_done, rl_ready,
     proj_added) = sems(
         "s_done max_ready exp_done t_done tile_high tile_low pv_done ot_ready proj_done rl_ready "
         "proj_added")
    (fold_done, fold_read, zeroed, kc_high) = sems(
         "fold_done fold_read zeroed kc_high")
    (g_bn, g_stats, rsg_var, g_rstd, g_z, g_zT, g_zT_ready, h_done, relu_ready, h_ready, y_done,
     lif_step, lif_done) = sems(
         "g_bn g_stats rsg_var g_rstd g_z g_zT g_zT_ready h_done relu_ready h_ready y_done lif_step "
         "lif_done")
    (c_bn, c_stats, c_var, c_rstd, c_z, c_zT, c_zT_ready, c_zT_low, c_zb, x_beta, sc_done, c_max, sc_read,
     pexp_ready, c_sum, pnorm_ready, tp_done, tp_act, pvc_done, res_ready, r_bn, r_stats, r_var, r_rstd,
     r_own, x3_ready, x3_copied, x3T_done, x3T_ready, lg_done, lg_ready, x3_stats, x3_meanvar, x3_var,
     x3_once) = sems(
         "c_bn c_stats c_var c_rstd c_z c_zT c_zT_ready c_zT_low c_zb x_beta sc_done c_max sc_read pexp_ready "
         "c_sum pnorm_ready tp_done tp_act pvc_done res_ready r_bn r_stats r_var r_rstd r_own "
         "x3_ready x3_copied x3T_done x3T_ready lg_done lg_ready x3_stats x3_meanvar x3_var x3_once")
    (wr_summed, oh_ready, rank_done, gexp_in, gexp_ready, slot_ready, expert_ready) = sems(
         "wr_summed oh_ready rank_done gexp_in gexp_ready slot_ready expert_ready")
    (e_z, e_zT, e_zT_ready, g1_done, he_act, he_dve, heT_done, heT_act, heT_dve, e_token, e_biased, g2_done,
     oe_ready) = sems(
         "e_z e_zT e_zT_ready g1_done he_act he_dve heT_done heT_act heT_dve e_token e_biased g2_done "
         "oe_ready")
    x_in = [sem(f"x_in{k}") for k in range(NG)]
    vw_out = [sem(f"vw_out{k}") for k in range(B)]
    xe_in = [sem(f"xe_in{k}") for k in range(4)]
    out_rows = [sem(f"out_rows{k}") for k in range(2)]

    VECS = 12
    ITEMS = S // P + 1
    UNITS = BG + 1
    LAST = ITEMS - 1
    MP = BG * H0
    key_rows = lambda j: P if j < KT - 1 else C

    def dve_norm(dve):
        own = Count(dve, dve_own)
        for g in range(NG):
            dve.wait_ge(x_in[g], 16)
            for i in range(GT * g, GT * g + GT):
                own.add(dve.bn_stats(stats[:, i, :], X[:, i, :]))
            own.wait()
            for i in range(GT * g, GT * g + GT):
                last = dve.bn_aggr(meanvar[:, i, :], stats[:, i, :])
            own.add(last)
            if g == 0:
                own.wait()
                dve.tensor_scalar(rs[:, 0, 0:GT], meanvar[:, 0:GT, 1], LN_EPS, None, ALU.add).then_inc(root_in, 1)
            if g == 1:
                dve.wait_ge(root_out, 1)
                normalized_twice(dve, own, meanvar[:, 0:GT, 1], rs[:, 0, 0:GT], rs[:, 1, 0:GT])
            if g == 2:
                dve.wait_ge(root_out, 2)
                own.add(dve.tensor_tensor(rstd[:, 0:GT], rs[:, 0, 0:GT], rs[:, 1, 0:GT], ALU.mult))
        dve.wait_ge(ctx_in, 16)
        for b in range(B):
            own.add(dve.bn_stats(stats[:, NT + b, :], ctxn[:, b, :]))
        own.wait()
        for b in range(B):
            last = dve.bn_aggr(meanvar[:, NT + b, :], stats[:, NT + b, :])
        own.add(last)
        own.wait()
        dve.engine_nop().then_inc(stats_ready, 1)

    def normalized_twice(dve, own, var, once, twice):
        own.add(dve.tensor_tensor(twice, var, once, ALU.mult))
        own.wait()
        own.add(dve.tensor_tensor(twice, twice, once, ALU.mult))
        own.wait()
        dve.tensor_scalar(twice, twice, LN_EPS, None, ALU.add).then_inc(root_in, 1)

    def pool_norm(pool):
        pool.wait_ge(half_set, 1)
        for i in range(2):
            pool.wait_ge(root_in, i + 1)
            pool.tensor_tensor(rs[:, i, 0:GT], rs[:, i, 0:GT], minus_half[:, 0:GT], ALU.pow).then_inc(root_out, 1)
        own = Count(pool, pool_own)
        pool.wait_ge(stats_ready, 1)
        var, once, twice = meanvar[:, GT:NT + B, 1], rs[:, 0, GT:NT + B], rs[:, 1, GT:NT + B]
        root = minus_half[:, GT:NT + B]
        for ins in (lambda: pool.tensor_scalar(once, var, LN_EPS, None, ALU.add),
                    lambda: pool.tensor_tensor(once, once, root, ALU.pow),
                    lambda: pool.tensor_tensor(twice, var, once, ALU.mult),
                    lambda: pool.tensor_tensor(twice, twice, once, ALU.mult),
                    lambda: pool.tensor_scalar(twice, twice, LN_EPS, None, ALU.add),
                    lambda: pool.tensor_tensor(twice, twice, root, ALU.pow)):
            own.add(ins())
            own.wait()
        pool.tensor_tensor(rstd[:, GT:NT], rs[:, 0, GT:NT], rs[:, 1, GT:NT], ALU.mult).then_inc(rstd_ready, 1)
        pool.tensor_copy(rstd[:, NT:NT + B], rs[:, 0, NT:NT + B]).then_inc(rstd_ready, 1)

    def normalize(dve, b, u):
        if u > 0:
            dve.wait_ge(zT_done, UNITS * b + u)
            dve.wait_ge(rstd_ready, 2)
        for s in range(GT if u < BG else 1):
            row = X[:, b * (S // P) + GT * u + s, :] if u < BG else ctxn[:, b, :]
            at = b * (S // P) + GT * u + s if u < BG else b + NT
            last = dve.tensor_scalar(Z[:, s, :], row, meanvar[:, at, 0:1], rstd[:, ds(at, 1)],
                                     ALU.subtract, ALU.mult)
        last.then_inc(z_ready, 1)

    def dve_project(dve, b):
        item = lambda i: b * ITEMS + i
        normalize(dve, b, 0)
        for i in range(ITEMS + 2):
            p = i % 2
            if i < ITEMS:
                dve.wait_ge(sq_ready, item(i) + 1)
                dve.tensor_reduce(ssum[:, p, :], sq[:, p, :].rearrange("p (h e) -> p h e", e=E0), AX.X, ALU.add) \
                   .then_inc(ssum_ready, 1)
                dve.wait_ge(ssum_ready, item(i) + 1)
                dve.tensor_scalar(rms2[:, p, :], ssum[:, p, :], 1.0 / E0, RMS_EPS ** 2, ALU.mult, ALU.max) \
                   .then_inc(rms_mean, 1)
                dve.wait_ge(v_high, item(i) + 1)
                v = PS[:, 5, 0:D].rearrange("p (h e) -> p h e", h=H0)
                dve.tensor_tensor(VHL[:, i, :, 1, :], v, VHL[:, i, :, 0, :].bitcast(F32), ALU.subtract).then_inc(v_low, 1)
            if i >= 2:
                j, s = i - 2, (i - 2) % GT
                dve.wait_ge(high_ready, item(j) + 1)
                if j < LAST:
                    low = QS[E0:P, j // GT, :, s * P:s * P + P]
                    dve.scalar_tensor_tensor(low, PS[E0:P, 6, :].rearrange("p (h n) -> p h n", h=H0), qgam[E0:P, :],
                                             low.bitcast(F32), ALU.mult, ALU.subtract)
                w = P if j < LAST else C + 1
                cols = slice(j * P, j * P + w)
                dve.scalar_tensor_tensor(KL[:, :, cols], PS[:, 7, :].rearrange("p (h n) -> p h n", h=H0)[:, :, 0:w],
                                         kgam[:, :], KH[:, :, cols].bitcast(F32), ALU.mult, ALU.subtract) \
                   .then_inc(low_ready, 1)
            if i < ITEMS:
                dve.wait_ge(rrms_ready, item(i) + 1)
                h = 2 * H0
                rows = PS[:, 2 + i % 3, :].rearrange("p (h e) -> p h e", e=E0)
                dve.tensor_tensor(qk2[:, p, :, :, :], rows.unsqueeze(2).to_broadcast([P, h, 2, E0]),
                                  rrms[:, p, :].unsqueeze(2).unsqueeze(3).to_broadcast([P, h, 2, E0]), ALU.mult) \
                   .then_inc(qk2_ready, 1)
            if i == 0 or i == GT:
                normalize(dve, b, 1 + i // GT)

    def act_project(act, b):
        item = lambda i: b * ITEMS + i

        def scale_rows(u):
            act.wait_ge(zT_done, UNITS * b + u + 1)
            n, g, c = (GN, lnlg, lnlb) if u < BG else (P, lnxg, lnxb)
            for k in range(KC):
                last = act.activation(lnT[:, k, 0:n], PS[:, k, 0:n], ACT.Identity, bias=c[:, k:k + 1],
                                      scale=g[:, k:k + 1])
            last.then_inc(lnT_ready, 1)

        scale_rows(0)
        for i in range(ITEMS + 2):
            p = i % 2
            if i < ITEMS:
                act.wait_ge(qkv_done, item(i) + 1)
                act.activation(sq[:, p, :], PS[:, 2 + i % 3, :], ACT.Square).then_inc(sq_ready, 1)
                act.wait_ge(v_done, item(i) + 1)
                act.activation(VHL[:, i, :, 0, :], PS[:, 5, 0:D].rearrange("p (h e) -> p h e", h=H0), ACT.Copy) \
                   .then_inc(v_high, 1)
            if i == 3:
                scale_rows(1)
            if i == 7:
                scale_rows(2)
            if i >= 2:
                j, s = i - 2, (i - 2) % GT
                act.wait_ge(qkT_done, item(j) + 1)
                if j < LAST:
                    act.activation(QS[:, j // GT, :, s * P:s * P + P], PS[:, 6, :].rearrange("p (h n) -> p h n", h=H0),
                                   ACT.Copy, scale=qgam[:, :])
                w = P if j < LAST else C + 1
                act.activation(KH[:, :, j * P:j * P + w],
                               PS[:, 7, :].rearrange("p (h n) -> p h n", h=H0)[:, :, 0:w],
                               ACT.Copy, scale=kgam[:, :]).then_inc(high_ready, 1)

    def pool_project(pool, b):
        for i in range(ITEMS):
            p = i % 2
            pool.wait_ge(rms_mean, b * ITEMS + i + 1)
            pool.tensor_tensor(rrms[:, p, :], rms2[:, p, :], minus_half[:, 0:2 * H0], ALU.pow).then_inc(rrms_ready, 1)
        for g in range(BG):
            wait_apart(pool, z_ready, UNITS * b + g + 1, waited_pool)
            for s in range(GT):
                row = X[:, b * (S // P) + GT * g + s, :]
                last = pool.tensor_tensor(row, row, boutb[:], ALU.add)
            last.then_inc(bias_added, 1)

    def pe_project(pe, b):
        item = lambda i: b * ITEMS + i

        def turn_rows(u):
            pe.wait_ge(z_ready, UNITS * b + u + 1)
            if u > 0:
                pe.wait_ge(lnT_ready, UNITS * b + u)
            for s in range(GT if u < BG else 1):
                for k in range(KC):
                    last = pe.transpose(PS[:, k, s * P:s * P + P], Z[:, s, k * P:k * P + P], ident[:])
            last.then_inc(zT_done, 1)

        def qkv(i):
            s, p = i % GT, i % 2
            pe.wait_ge(lnT_ready, UNITS * b + i // GT + 1)
            if i >= 3:
                pe.wait_ge(qk2_ready, item(i) - 2)
            for k in range(KC):
                last = pe.matmul(PS[:, 2 + i % 3, :], lnT[:, k, s * P:s * P + P], wqkv[:, k, 0:2 * D],
                                 start=k == 0, stop=k == KC - 1)
            last.then_inc(qkv_done, 1)
            if i >= 1:
                pe.wait_ge(v_low, item(i))
            for k in range(KC):
                last = pe.matmul(PS[:, 5, 0:D], lnT[:, k, s * P:s * P + P], wqkv[:, k, 2 * D:3 * D],
                                 start=k == 0, stop=k == KC - 1)
            last.then_inc(v_done, 1)

        def turn_heads(i):
            pe.wait_ge(qk2_ready, item(i) + 1)
            if i >= 1:
                pe.wait_ge(low_ready, item(i))
            for h in range(0 if i < LAST else H0, 2 * H0):
                last = pe.transpose(PS[:, 6 + h // H0, (h % H0) * P:(h % H0) * P + P],
                                    qk2[:, i % 2, h, :, :].rearrange("p a e -> p (a e)"), ident[:])
            last.then_inc(qkT_done, 1)

        turn_rows(0)
        for i in range(ITEMS + 2):
            if i < ITEMS:
                qkv(i)
            if i == 3 or i == 7:
                turn_rows(1 + i // GT)
            if i >= 2:
                turn_heads(i - 2)

    SCORES_AT = (0, 5 * 512 - KPAD)
    KEY_CHUNKS = []
    for at in SCORES_AT:
        cuts = [at] + [c for c in range(512, 5 * 512, 512) if at < c < at + KPAD] + [at + KPAD]
        KEY_CHUNKS.append([(c0 // 512, c0 % 512, c0 - at, c1 - at) for c0, c1 in zip(cuts, cuts[1:])])
    SHARED = 2
    TURNS = []
    for m in range(MP):
        order = [0, 1, 2, "out 0", 3, 4, 5, "out 1", 6, 7, 8]
        TURNS += [(m, x) if isinstance(x, int) else (m - 1, x) for x in order if isinstance(x, int) or m > 0]
    TURNS += [(MP - 1, "out 0"), (MP - 1, "out 1")]
    bank_of = lambda m, x: 5 + TURNS.index((m, x)) % 2

    def pe_attend(pe, b):
        def wait_bank(m, x):
            at = TURNS.index((m, x))
            if at >= 2:
                m0, x0 = TURNS[at - 2]
                if isinstance(x0, int):
                    pe.wait_ge(tile_low, KT * (MP * b + m0) + x0 + 1)
                else:
                    pe.wait_ge(proj_added, GT * (MP * b + m0) + (2 if x0 == "out 0" else 4))

        def scores(m, s, shared):
            g, h, p = m // H0, m % H0, s % 2
            at = GT * m + s
            if at >= 2:
                pe.wait_ge(exp_done, GT * MP * b + at - 1)
            else:
                pe.wait_ge(low_ready, ITEMS * b + ITEMS)
                pe.wait_ge(v_low, ITEMS * b + ITEMS)
            q = QS[:, g, h, s * P:s * P + P]
            for bank, c, k0, k1 in KEY_CHUNKS[p]:
                if (bank == SHARED) == shared:
                    masked = k1 == KPAD
                    for k in (KH, KL):
                        last = pe.matmul(PS[:, bank, c:c + k1 - k0], q, k[:, h, k0:k1], start=k is KH,
                                         stop=k is KL and not masked)
                    if masked:
                        c += S - k0
                        last = pe.matmul(PS[:, bank, c:c + C + 1], ones33[0:1, :], maskr[0:1, b, :], start=False, stop=True)
            return last

        def own_scores(m, s):
            scores(m, s, False)

        def shared_scores(m, pair):
            if GT * m + 2 * pair >= 2:
                pe.wait_ge(exp_done, GT * MP * b + GT * m + 2 * pair)
            scores(m, 2 * pair, True)
            scores(m, 2 * pair + 1, True).then_inc(s_done, 1)

        def project_out(m, half):
            n, h, x = MP * b + m, m % H0, f"out {half}"
            wait_bank(m, x)
            if half == 0:
                pe.wait_ge(ot_ready, n + 1)
                pe.wait_ge(wout_scaled, 1)
            for s in (2 * half, 2 * half + 1):
                last = pe.matmul(PS[:, bank_of(m, x), s % 2 * D:s % 2 * D + D], OT[:, m % 2, s * P:s * P + P],
                                 wout[:, h, :], start=True, stop=True)
            last.then_inc(proj_done, 1)

        def turn_probs(m, j):
            n = MP * b + m
            wait_bank(m, j)
            for s in range(GT):
                if j == 0:
                    pe.wait_ge(exp_done, GT * n + s + 1)
                last = pe.transpose(PS[0:key_rows(j), bank_of(m, j), s * P:s * P + P],
                                    prob[:, m % 2, s, j * P:j * P + key_rows(j)], ident[:])
            last.then_inc(t_done, 1)

        def values(m, j):
            n, h, r = MP * b + m, m % H0, key_rows(j)
            if j == 0 and m > 0:
                pe.wait_ge(ot_ready, n)
            at = (KT * m + j) % PB
            pe.wait_ge(tile_low, KT * n + j + 1)
            v = VHL[0:r, j, h, :, :].rearrange("p a e -> p (a e)")
            pe.matmul(PS[:, 7, :], v, PH[0:r, at, :], start=j == 0, stop=False)
            pe.matmul(PS[:, 7, :], v, PL[0:r, at, :], start=False, stop=j == KT - 1).then_inc(pv_done, 1)

        for pair in range(2):
            own_scores(0, 2 * pair)
            own_scores(0, 2 * pair + 1)
            shared_scores(0, pair)
        for m in range(MP):
            own = (lambda s: own_scores(m + 1, s)) if m + 1 < MP else (lambda s: None)
            shared = (lambda pair: shared_scores(m + 1, pair)) if m + 1 < MP else (lambda pair: None)
            out = (lambda half: project_out(m - 1, half)) if m > 0 else (lambda half: None)
            own(0)
            turn_probs(m, 0)
            turn_probs(m, 1)
            own(1)
            shared(0)
            if m > 0:
                values(m - 1, 7)
                values(m - 1, 8)
            turn_probs(m, 2)
            values(m, 0)
            out(0)
            values(m, 1)
            turn_probs(m, 3)
            own(2)
            turn_probs(m, 4)
            own(3)
            shared(1)
            values(m, 2)
            turn_probs(m, 5)
            values(m, 3)
            out(1)
            turn_probs(m, 6)
            values(m, 4)
            turn_probs(m, 7)
            values(m, 5)
            turn_probs(m, 8)
            values(m, 6)
        values(MP - 1, KT - 2)
        values(MP - 1, KT - 1)
        for half in range(2):
            project_out(MP - 1, half)

    def dve_attend(dve, b):
        def row_max(m, s):
            at = SCORES_AT[s % 2]
            dve.wait_ge(s_done, 2 * (MP * b + m) + s // 2 + 1)
            dve.tensor_reduce(nmax[:, m % 2, s:s + 1], PSf[:, at:at + KEYS], AX.X, ALU.max, negate=True) \
               .then_inc(max_ready, 1)

        def low_part(m, j):
            n, r, at = MP * b + m, key_rows(j), (KT * m + j) % PB
            dve.wait_ge(tile_high, KT * n + j + 1)
            dve.tensor_tensor(PL[0:r, at, :], PS[0:r, bank_of(m, j), :], PH[0:r, at, :].bitcast(F32), ALU.subtract) \
               .then_inc(tile_low, 1)

        def reciprocals(m):
            dve.wait_ge(exp_done, GT * (MP * b + m) + GT)
            dve.reciprocal(rl[:, m % 2, :], lsum[:, m % 2, :]).then_inc(rl_ready, 1)

        def add_out(m, half):
            n, g = MP * b + m, m // H0
            dve.wait_ge(proj_done, 2 * n + half + 1)
            if half == 0:
                dve.wait_ge(rl_ready, n + 1)
            for s in (2 * half, 2 * half + 1):
                if m % H0 == 0:
                    dve.wait_ge(bias_added, BG * b + g + 1)
                else:
                    dve.wait_ge(proj_added, GT * n - GT + s + 1)
                row = X[:, b * (S // P) + GT * g + s, :]
                dve.scalar_tensor_tensor(row, PS[:, bank_of(m, f"out {half}"), s % 2 * D:s % 2 * D + D],
                                         rl[:, m % 2, s:s + 1], row, ALU.mult, ALU.add).then_inc(proj_added, 1)

        for s in range(GT):
            row_max(0, s)
        for m in range(MP):
            nxt = (lambda s: row_max(m + 1, s)) if m + 1 < MP else (lambda s: None)
            out = (lambda half: add_out(m - 1, half)) if m > 0 else (lambda half: None)
            low_part(m, 0)
            low_part(m, 1)
            nxt(0)
            nxt(1)
            low_part(m, 2)
            out(0)
            low_part(m, 3)
            low_part(m, 4)
            nxt(2)
            nxt(3)
            low_part(m, 5)
            out(1)
            low_part(m, 6)
            reciprocals(m)
            low_part(m, 7)
            low_part(m, 8)
        for half in range(2):
            add_out(MP - 1, half)

    def act_attend(act, b):
        def exps(m, s):
            at = SCORES_AT[s % 2]
            act.wait_ge(max_ready, GT * (MP * b + m) + s - s % 2 + 2)
            act.activation(prob[:, m % 2, s, :], PSf[:, at:at + KEYS], ACT.Exp,
                           bias=nmax[:, m % 2, s:s + 1], accum_out=lsum[:, m % 2, s:s + 1]).then_inc(exp_done, 1)

        def high_part(m, j):
            n, r, at = MP * b + m, key_rows(j), (KT * m + j) % PB
            act.wait_ge(t_done, KT * n + j + 1)
            act.wait_ge(pv_done, KT * n + j + 1)
            act.activation(PH[0:r, at, :], PS[0:r, bank_of(m, j), :], ACT.Copy).then_inc(tile_high, 1)

        def copy_out(m):
            act.wait_ge(pv_done, KT * (MP * b + m) + KT + PB)
            act.activation(OT[:, m % 2, :], PS[:, 7, :], ACT.Copy).then_inc(ot_ready, 1)

        for s in range(GT):
            exps(0, s)
        for m in range(MP):
            nxt = (lambda s: exps(m + 1, s)) if m + 1 < MP else (lambda s: None)
            high_part(m, 0)
            high_part(m, 1)
            if m > 0:
                copy_out(m - 1)
            high_part(m, 2)
            nxt(0)
            nxt(1)
            high_part(m, 3)
            high_part(m, 4)
            high_part(m, 5)
            nxt(2)
            high_part(m, 6)
            nxt(3)
            high_part(m, 7)
            high_part(m, 8)
        copy_out(MP - 1)

    ctx_chunks = [(c0, min(c0 + P, HK)) for c0 in range(0, HK, P)]

    def pe_fold(pe):
        bank, vw_bank = Ring(pe, fold_done, fold_read, FOLD_BANKS), Ring(pe, vwo_done, vwo_read, VWO_BANKS)
        pe.wait_ge(proj_added, GT * MP * B)
        pe.wait_ge(ctx_in, 16)
        pe.wait_ge(fold_in, 16 * 4)
        k0 = bank.to_fill()
        for k in range(KC):
            for b in range(B):
                last = pe.transpose(PS[:, k0, (k * B + b) * P:(k * B + b) * P + P], ctxn[:, b, k * P:k * P + P], ident[:])
        bank.filled(last)
        for c2 in range(0, FC, 2):
            k0 = bank.to_fill()
            for c in range(2):
                for k in range(KC):
                    at = (c * KC + k) * P
                    last = pe.transpose(PS[:, k0, at:at + P], wq1[:, k, (c2 + c) * P:(c2 + c) * P + P], ident[:])
            bank.filled(last)
        pe.wait_ge(fold_read, 1)
        for w in (wk1, wv1):
            for c in range(FC):
                k0 = bank.to_fill()
                for k in range(KC):
                    last = pe.matmul(PS[:, k0, 0:B * C], w[:, k, c * P:c * P + P],
                                     ctxT[:, k, :, :].rearrange("p b c -> p (b c)"), start=k == 0, stop=k == KC - 1)
                bank.filled(last)
        def values_times_wo(b, h):
            k0, c, lo = vw_bank.to_fill(), h // 2, slice(h % 2 * E0, h % 2 * E0 + E0)
            vw_bank.filled(pe.matmul(PS[0:C, k0, 0:D], valsT[lo, c, b, :], wo1[lo, c, :], start=True, stop=True))

        pe.wait_ge(zeroed, 3)
        for c in range(FC):
            rhs = keysT[:, c, :, :, :].rearrange("p b a c -> p (b a c)")
            pe.wait_ge(fold_read, 1 + FC // 2 + c + 1)
            for k in range(KC):
                k0 = bank.to_fill()
                bank.filled(pe.matmul(PS[:, k0, 0:2 * B * C], wqT[:, c, k * P:k * P + P], rhs, start=True, stop=True))
            k0 = bank.to_fill()
            bank.filled(pe.matmul(PS[0:33, k0, 0:2 * B * C], bqz[:, c, :], rhs, start=True, stop=True))
            pe.wait_ge(fold_read, 1 + FC // 2 + FC + c + 1)
            for a in range(2):
                values_times_wo(0, 2 * c + a)
        pe.wait_ge(ffn_in, 32)
        for k in range(KC):
            for c4 in range(0, FC, 4):
                k0 = bank.to_fill()
                for c in range(4):
                    last = pe.transpose(PS[:, k0, c * P:c * P + P], wfc[:, c4 + c, k * P:k * P + P], ident[:])
                bank.filled(last)
        for c2 in range(0, FC, 2):
            k0 = bank.to_fill()
            for c in range(2):
                for k in range(KC):
                    at = (c * KC + k) * P
                    last = pe.transpose(PS[:, k0, at:at + P], wproj[:, k, (c2 + c) * P:(c2 + c) * P + P], ident[:])
            bank.filled(last)
            for h in range(2 * c2, 2 * c2 + 4):
                values_times_wo(1, h)

    def act_fold(act):
        vw_bank = Ring(act, vwo_done, vwo_read, VWO_BANKS)
        for b in range(B):
            if b > 0:
                act.wait_ge(vw_out[b - 1], 16)
            for h in range(H1):
                k0 = vw_bank.to_read()
                vw_bank.read(act.activation(vwn[:, h, :], PS[0:C, k0, 0:D], ACT.Copy))

    def dve_fold(dve):
        bank, own = Ring(dve, fold_done, fold_read, FOLD_BANKS), Count(dve, fold_own)
        dve.wait_ge(proj_added, GT * MP * B)
        dve.wait_ge(pv_done, KT * MP * B + PB)
        dve.wait_ge(l1_in, 48)
        dve.memset(bqz[:], 0.0).then_inc(zeroed, 1)
        k0 = bank.to_read()
        bank.read(dve.tensor_copy(ctxT[:].rearrange("p k b c -> p (k b) c"),
                                  PS[:, k0, :].rearrange("p (a n) -> p a n", n=P)[:, :, 0:C]))
        for c2 in range(0, FC, 2):
            k0 = bank.to_read()
            bank.read(dve.tensor_copy(wqT[:, c2:c2 + 2, :], PS[:, k0, :].rearrange("p (c n) -> p c n", c=2)))
        dve.wait_ge(zeroed, 2)
        for col in (0, 32):
            last = dve.tensor_copy(bqz[:, :, col], bq1[:])
        last.then_inc(zeroed, 1)
        for c in range(FC):
            k0 = bank.to_read()
            for a in range(2):
                lo = slice(a * E0, a * E0 + E0)
                last = dve.tensor_scalar(keysT[lo, c, :, a, :], PS[lo, k0, 0:B * C].rearrange("p (b c) -> p b c", b=B),
                                         bk1[lo, c:c + 1], E0 ** -0.5, ALU.add, ALU.mult)
            bank.read(last)
        for c in range(FC):
            k0 = bank.to_read()
            bank.read(dve.tensor_scalar(valsT[:, c, :, :], PS[:, k0, 0:B * C].rearrange("p (b c) -> p b c", b=B),
                                        bv1[:, c:c + 1], None, ALU.add))
        for c in range(FC):
            cols = slice(2 * C * c, 2 * C * c + 2 * C)
            for k in range(KC):
                k0 = bank.to_read()
                product = PS[:, k0, 0:2 * B * C].rearrange("p (b n) -> p b n", b=B)
                own.add(dve.tensor_copy(kwH[:, k, :, cols], product))
                own.wait()
                bank.read(dve.tensor_tensor(kwL[:, k, :, cols], product, kwH[:, k, :, cols].bitcast(F32), ALU.subtract))
            k0 = bank.to_read()
            sums = PS[:, k0, 0:2 * B * C].rearrange("p (b n) -> p b n", b=B)
            dve.tensor_copy(kc[:, :, cols], sums[0:33]).then_inc(kc_high, 1)
            dve.wait_ge(kc_high, c + 1)
            bank.read(dve.tensor_tensor(kc[32:33, :, cols], sums[32:33], kc[32:33, :, cols].bitcast(F32), ALU.subtract))

        ffn_norm(dve, 0)
        for k in range(KC):
            for c4 in range(0, FC, 4):
                k0 = bank.to_read()
                high, low = (w[:, k, c4 * P:c4 * P + 4 * P] for w in (wfcH, wfcL))
                own.add(dve.tensor_copy(high, PS[:, k0, :]))
                own.wait()
                bank.read(dve.tensor_tensor(low, PS[:, k0, :], high.bitcast(F32), ALU.subtract))
        for c2 in range(0, FC, 2):
            k0 = bank.to_read()
            bank.read(dve.tensor_copy(wprojT[:, c2:c2 + 2, :], PS[:, k0, :].rearrange("p (c n) -> p c n", c=2)))

    FOLD_BANKS, VWO_BANKS = [0, 1, 2, 3, 4], [5, 6, 7]
    FOLD_ALL = 1 + FC // 2 + 2 * FC + 3 * FC + FC

    def sp_fold(sp):
        sp.wait_ge(proj_added, GT * MP * B)
        sp.dma_start(wfc, t["L0_ffn_W_fc"].rearrange("(c p) d -> p c d", p=P)).then_inc(ffn_in, 16)
        sp.dma_start(wproj, t["L0_ffn_W_proj"].rearrange("(k p) f -> p k f", p=P)).then_inc(ffn_in, 16)
        for b in range(B):
            sp.wait_ge(vwo_read, H1 * b + H1)
            rows = t["vw_rows"][b]
            sp.dma_start(rows.rearrange("(h c) n -> c h n", c=C), vwn[:]).then_inc(vw_out[b], 16)
            sp.wait_ge(vw_out[b], 16)
            whole = HK // P
            sp.dma_start(vw[:, b, 0:whole, :], rows[0:whole * P, :].rearrange("(t p) n -> p t n", p=P)).then_inc(vw_in, 16)
            sp.dma_start(vw[0:HK - whole * P, b, whole, :], rows[whole * P:HK, :]).then_inc(vw_in, 16)

    EDGES = spike_edges()

    def pe_ffn(pe):
        def turn(g):
            pe.wait_ge(g_z, g + 1)
            for s in range(GT):
                for k in range(KC):
                    last = pe.transpose(PS[:, k, s * P:s * P + P], Z[:, s, k * P:k * P + P], ident[:])
            last.then_inc(g_zT, 1)

        def group(g, last_group):
            pe.wait_ge(g_zT_ready, g + 1)
            pe.wait_ge(g_zT_low, g + 1)
            for c in range(FC):
                if c >= 2:
                    pe.wait_ge(relu_ready, FC * g + c - 1)
                products = [(w[:, k, c * P:c * P + P], z[:, k, :])
                            for w, z in ((wfcH, zTH), (wfcH, zTL), (wfcL, zTH)) for k in range(KC)]
                for i, (w, z) in enumerate(products):
                    last = pe.matmul(PS[:, 2 + c % 2, :], w, z, start=i == 0, stop=i == len(products) - 1)
                last.then_inc(h_done, 1)
            if not last_group:
                turn(g + 1)
            pe.wait_ge(h_ready, FC * g + FC)
            pe.wait_ge(lif_done, 2 * g + 1)
            for half in range(2):
                if half == 1:
                    pe.wait_ge(lif_done, 2 * g + 2)
                for s in range(2):
                    at = (2 * half + s) * P
                    for c in range(FC):
                        last = pe.matmul(PS[:, 4 + half, s * D:s * D + D], hT[:, c, at:at + P], wprojT[:, c, :],
                                         start=c == 0, stop=c == FC - 1)
                last.then_inc(y_done, 1)
        pe.wait_ge(fold_read, FOLD_ALL)
        pe.wait_ge(vwo_read, H1 * B)
        turn(0)
        with pe.Fori(0, NG - 1) as g:
            group(g, False)
        group(NG - 1, True)

    def act_ffn(act):
        def copy_turned(g):
            act.wait_ge(g_zT, g + 1)
            for k in range(KC):
                last = act.activation(zTH[:, k, :], PS[:, k, :], ACT.Copy)
            last.then_inc(g_zT_ready, 1)

        def group(g, last_group):
            for c in range(FC):
                act.wait_ge(h_done, FC * g + c + 1)
                act.activation(relu[:, c % 2, :], PS[:, 2 + c % 2, :], ACT.Relu).then_inc(relu_ready, 1)
                if c == 0:
                    act.wait_ge(y_done, 2 * g + 1)
                act.wait_ge(relu_ready, FC * g + c + 1)
                act.activation(hT[:, c, :], relu[:, c % 2, :], ACT.Square).then_inc(h_ready, 1)
            if not last_group:
                copy_turned(g + 1)
        copy_turned(0)
        with act.Fori(0, NG - 1) as g:
            group(g, False)
        group(NG - 1, True)

    def pool_ffn(pool):
        with pool.Fori(0, NG) as g:
            wait_apart(pool, g_stats, g + 1, waited_pool)
            pool.tensor_scalar(rsg[:], mvg[:, :, 1], LN_EPS, None, ALU.add).then_inc(rsg_var, 1)
            pool.wait_ge(rsg_var, g + 1)
            pool.tensor_tensor(rsg[:], rsg[:], minus_half[:, 0:GT], ALU.pow).then_inc(g_rstd, 1)

    def ffn_norm(dve, g):
        for s in range(GT):
            last = dve.bn_stats(stg[:, s, :], X[:, GT * g + s, :])
        last.then_inc(g_bn, 1)
        wait_apart(dve, g_bn, g + 1, waited_dve)
        for s in range(GT):
            last = dve.bn_aggr(mvg[:, s, :], stg[:, s, :])
        last.then_inc(g_stats, 1)
        dve.wait_ge(g_rstd, g + 1)
        for s in range(GT):
            last = dve.tensor_scalar(Z[:, s, :], X[:, GT * g + s, :], mvg[:, s, 0:1], rsg[:, s:s + 1],
                                     ALU.subtract, ALU.mult)
        last.then_inc(g_z, 1)

    def dve_ffn(dve):
        def z_low(g):
            dve.wait_ge(g_zT_ready, g + 1)
            for k in range(KC):
                last = dve.tensor_tensor(zTL[:, k, :], PS[:, k, :], zTH[:, k, :].bitcast(F32), ALU.subtract)
            last.then_inc(g_zT_low, 1)

        def spike(g, halves=range(2)):
            for half in halves:
                dve.wait_ge(y_done, 2 * g + half + 2)
                dve.wait_ge(lif_done, 2 * g + half + 2)
                y = PS[:, 4 + half, :]
                dve.tensor_scalar(spikes[:], y, EDGES[0], None, ALU.is_gt).then_inc(lif_step, 1)
                for n, edge in enumerate(EDGES[1:]):
                    dve.wait_ge(lif_step, 5 * (2 * g + half) + n + 1)
                    last = dve.scalar_tensor_tensor(spikes[:], y, edge, spikes[:], ALU.is_gt, ALU.add)
                    last.then_inc(lif_step, 1)
                dve.wait_ge(lif_step, 5 * (2 * g + half) + 5)
                x2 = X[:, ds(GT * g + 2 * half, 2), :]
                dve.scalar_tensor_tensor(x2, spikes[:].rearrange("p (s d) -> p s d", d=D), tg5[:], x2,
                                         ALU.mult, ALU.add).then_inc(lif_done, 1)
        z_low(0)
        with dve.Fori(0, NG - 1) as g:
            dve.wait_ge(g_zT, g + 1)
            ffn_norm(dve, g + 1)
            z_low(g + 1)
            spike(g)
        cross_norm(dve, 0)
        cross_norm(dve, 1)
        spike(NG - 1, [0])
        cross_z_low(dve, 0, 0)
        spike(NG - 1, [1])

    SCORES = [(c0, min(c0 + 512, HK)) for c0 in range(0, HK, 512)]
    TB = S // P
    PAIRS = TB // 2
    HEADS_A = 512 // C
    PARTS = [(0, HEADS_A), (HEADS_A, H1)]

    def pairs(eng, body):
        for b in range(B):
            for p in range(2):
                body(b, TB * b + p, p)
            with eng.Fori(1, PAIRS - 1) as i:
                for p in range(2):
                    body(b, i * 2 + (TB * b + p), p)
            for p in range(2):
                body(b, TB * b + TB - 2 + p, p)

    exists = lambda n: not isinstance(n, int) or 0 <= n < NT

    def pe_cross(pe):
        def turn(n, p):
            pe.wait_ge(c_z, n + 1)
            if exists(n - 1):
                pe.wait_ge(c_zT_low, n)
            for k in range(KC):
                last = pe.transpose(PS[:, 0, k * P:k * P + P], zc[:, p, k * P:k * P + P], ident[:])
            last.then_inc(c_zT, 1)

        def scores(n, b, p):
            pe.wait_ge(c_zT_low, n + 1)
            if exists(n - 1):
                pe.wait_ge(sc_read, 2 * n)
            for i, (c0, c1) in enumerate(SCORES):
                for z, w in ((zcH, kwH), (zcH, kwL), (zcL, kwH)):
                    for k in range(KC):
                        pe.matmul(PS[:, 1 + i, 0:c1 - c0], z[:, p, k * P:k * P + P], w[:, k, b, c0:c1],
                                  start=w is kwH and z is zcH and k == 0, stop=False)
                last = pe.matmul(PS[:, 1 + i, 0:c1 - c0], ones33[:], kc[:, b, c0:c1], start=False, stop=True)
                if i == 0 or i == len(SCORES) - 1:
                    last.then_inc(sc_done, 1)

        def turn_probs(n, p):
            pe.wait_ge(pnorm_ready, 2 * n + 2)
            for c, (c0, c1) in enumerate(ctx_chunks):
                ins = pe.transpose(PS[0:c1 - c0, 4 + c // 4, c % 4 * P:c % 4 * P + P], pc[:, p, c0:c1], ident[:])
            ins.then_inc(tp_done, 1)

        def values(n, b, p):
            if exists(n - 1):
                pe.wait_ge(res_ready, n)
            pe.wait_ge(tp_act, 4 * n + 4)
            for c, (c0, c1) in enumerate(ctx_chunks):
                r = c1 - c0
                ins = pe.matmul(PS[:, 7, 0:D], pcT[0:r, c, :], vw[0:r, b, c, :], start=c == 0, stop=c == HC - 1)
            ins.then_inc(pvc_done, 1)

        def turn_x3(n, p):
            pe.wait_ge(x3_ready, n + 1)
            if exists(n - 1):
                pe.wait_ge(x3T_ready, n)
            pe.wait_ge(c_zT_low, n + 3 if exists(n + 3) and exists(n + 2) else NT)
            for k in range(KC):
                last = pe.transpose(PS[:, 0, D + k * P:D + k * P + P], x3[:, p, k * P:k * P + P], ident[:])
            last.then_inc(x3T_done, 1)

        def logits(n, p):
            pe.wait_ge(x3T_ready, n + 1)
            pe.wait_ge(lg_ready, n + 1)
            if exists(n + 1):
                pe.wait_ge(res_ready, n + 2)
            for k in range(KC):
                last = pe.matmul(PS[:, 7, D:D + E], x3T[:, p, k * P:k * P + P], wr[:, k, :], start=k == 0, stop=k == KC - 1)
            last.then_inc(lg_done, 1)

        def body(b, n, p):
            turn_probs(n, p)
            if exists(n + 1):
                scores(n + 1, b if not isinstance(n, int) else (n + 1) // TB, 1 - p)
            if exists(n - 2):
                logits(n - 2, p)
            values(n, b, p)
            if exists(n - 1):
                turn_x3(n - 1, 1 - p)
            if exists(n + 2):
                turn(n + 2, p)

        pe.wait_ge(relu_ready, FC * NG)
        turn(0, 0)
        scores(0, 0, 0)
        turn(1, 1)
        pe.wait_ge(lif_done, 2 * NG + 2)
        pe.wait_ge(vw_in, 16 * 2 * B)
        pe.wait_ge(cross_in, 16 * CROSS_LOADS)
        pairs(pe, body)
        turn_x3(NT - 1, 1)
        logits(NT - 2, 0)
        logits(NT - 1, 1)

    def row_stats(dve, n, p):
        if exists(n - 2):
            dve.wait_ge(c_z, n - 1)
        dve.bn_stats(st1[:, 0, p, :], X[:, n, :]).then_inc(c_bn, 1)
        wait_apart(dve, c_bn, n + 1, waited_dve)
        dve.bn_aggr(mv1[:, 0, p, :], st1[:, 0, p, :]).then_inc(c_stats, 1)

    def normalize_rows(dve, n, p):
        dve.wait_ge(c_rstd, n + 1)
        if exists(n - 2):
            dve.wait_ge(c_zT, n - 1)
            dve.wait_ge(c_zb, n - 1)
        dve.tensor_scalar(zc[:, p, :], X[:, n, :], mv1[:, 0, p, 0:1], rs1[:, 0, p:p + 1],
                          ALU.subtract, ALU.mult).then_inc(c_z, 1)

    def cross_z_low(dve, n, p):
        dve.wait_ge(c_zT_ready, n + 1)
        if exists(n - 3):
            dve.wait_ge(x3T_ready, n - 2)
        dve.tensor_tensor(zcL[:, p, :], PS[:, 0, 0:D], zcH[:, p, :].bitcast(F32), ALU.subtract).then_inc(c_zT_low, 1)

    def cross_norm(dve, n):
        row_stats(dve, n, n)
        normalize_rows(dve, n, n)

    by_head = lambda v, p, h0, h1: v[:, p, h0:h1].unsqueeze(2).to_broadcast([P, h1 - h0, C])

    def dve_cross(dve):
        def subtract_max(n, p, part):
            h0, h1 = PARTS[part]
            sc = PSf[:, 512 + h0 * C:512 + h1 * C].rearrange("p (h c) -> p h c", c=C)
            pr = pc[:, p, h0 * C:h1 * C].rearrange("p (h c) -> p h c", c=C)
            dve.wait_ge(sc_done, 2 * n + part + 1)
            dve.tensor_reduce(mx1[:, p, h0:h1], sc, AX.X, ALU.max).then_inc(c_max, 1)
            dve.wait_ge(c_max, 2 * n + part + 1)
            dve.tensor_tensor(pr, sc, by_head(mx1, p, h0, h1), ALU.subtract).then_inc(sc_read, 1)

        def divide_by_sum(n, p, part):
            h0, h1 = PARTS[part]
            pr = pc[:, p, h0 * C:h1 * C].rearrange("p (h c) -> p h c", c=C)
            dve.wait_ge(pexp_ready, 2 * n + part + 1)
            dve.tensor_reduce(sum1[:, p, h0:h1], pr, AX.X, ALU.add).then_inc(c_sum, 1)
            dve.wait_ge(c_sum, 4 * n + 2 * part + 1)
            dve.reciprocal(sum1[:, p, h0:h1], sum1[:, p, h0:h1]).then_inc(c_sum, 1)
            if part == 1:
                dve.wait_ge(c_sum, 4 * n + 2 * part + 2)
                dve.tensor_tensor(pr, pr, by_head(sum1, p, h0, h1), ALU.mult).then_inc(pnorm_ready, 1)

        def residual(n, p):
            dve.wait_ge(pvc_done, n + 1)
            dve.wait_ge(c_zb, n + 1)
            if exists(n - 2):
                dve.wait_ge(x3_ready, n - 1)
            dve.tensor_tensor(resid[:, p, :], PS[:, 7, 0:D], zbo[:, p, :], ALU.add).then_inc(res_ready, 1)

        def residual_stats(n, p):
            dve.wait_ge(res_ready, n + 1)
            dve.bn_stats(st1[:, 1, p, :], resid[:, p, :]).then_inc(r_bn, 1)
            wait_apart(dve, r_bn, n + 1, waited_dve)
            dve.bn_aggr(mv1[:, 1, p, :], st1[:, 1, p, :]).then_inc(r_stats, 1)

        def x3_variance(n, p):
            wait_apart(dve, x3_stats, n + 2, waited_dve)
            wait_apart(dve, x3_var, 2 * n + 2, waited_dve)
            dve.bn_aggr(mv3[:, p, :], st3[:, p, :]).then_inc(x3_meanvar, 1)
            dve.wait_ge(x3_meanvar, n + 1)
            dve.tensor_copy(meanvar[:, n, :], mv3[:, p, :]).then_inc(x3_var, 1)
            dve.tensor_scalar(rs[:, 0, ds(n, 1)], mv3[:, p, 1:2], LN_EPS, None, ALU.add).then_inc(x3_var, 1)

        def add_norm(n, p):
            dve.wait_ge(r_rstd, n + 1)
            dve.tensor_scalar(resid[:, p, :], resid[:, p, :], mv1[:, 1, p, 0:1], rs1[:, 1, p:p + 1],
                              ALU.subtract, ALU.mult).then_inc(r_own, 1)
            dve.wait_ge(r_own, 2 * n + 1)
            dve.tensor_tensor(resid[:, p, :], resid[:, p, :], lngb[:], ALU.mult).then_inc(r_own, 1)
            dve.wait_ge(r_own, 2 * n + 2)
            dve.wait_ge(x_beta, n + 1)
            if exists(n - 1):
                dve.wait_ge(x3T_done, n)
                dve.wait_ge(x3_copied, n)
                dve.wait_ge(x3_stats, n)
            dve.tensor_tensor(x3[:, p, :], X[:, n, :], resid[:, p, :], ALU.add).then_inc(x3_ready, 1)

        def keep_logits(n, p):
            dve.wait_ge(lg_done, n + 1)
            dve.tensor_copy(LG[:, n, :], PS[:, 7, D:D + E]).then_inc(lg_ready, 1)
            dve.wait_ge(x3_ready, n + 1)
            dve.bn_stats(st3[:, p, :], x3[:, p, :]).then_inc(x3_stats, 1)

        def body(b, n, p):
            if exists(n + 2):
                row_stats(dve, n + 2, p)
            if exists(n - 1):
                add_norm(n - 1, 1 - p)
            if exists(n + 1):
                subtract_max(n + 1, 1 - p, 0)
                subtract_max(n + 1, 1 - p, 1)
                divide_by_sum(n + 1, 1 - p, 0)
            if exists(n + 2):
                normalize_rows(dve, n + 2, p)
            if exists(n + 1):
                divide_by_sum(n + 1, 1 - p, 1)
            residual(n, p)
            if exists(n - 2):
                keep_logits(n - 2, p)
            if exists(n + 2):
                cross_z_low(dve, n + 2, p)
            residual_stats(n, p)
            if exists(n - 2):
                x3_variance(n - 2, p)

        for part in range(2):
            subtract_max(0, 0, part)
        cross_z_low(dve, 1, 1)
        for part in range(2):
            divide_by_sum(0, 0, part)
        pairs(dve, body)
        add_norm(NT - 1, 1)
        for n in (NT - 2, NT - 1):
            keep_logits(n, n % 2)
            x3_variance(n, n % 2)

    def act_cross(act):
        def copy_turned(n, p):
            act.wait_ge(c_zT, n + 1)
            if exists(n - 3):
                act.wait_ge(x3T_done, n - 2)
            act.activation(zcH[:, p, :], PS[:, 0, 0:D], ACT.Copy).then_inc(c_zT_ready, 1)

        def numerators(n, p, part):
            h0, h1 = PARTS[part]
            act.wait_ge(sc_read, 2 * n + part + 1)
            pr = pc[:, p, h0 * C:h1 * C]
            act.activation(pr, pr, ACT.Exp).then_inc(pexp_ready, 1)

        def copy_x3T(n, p):
            act.wait_ge(x3T_done, n + 1)
            act.activation(x3T[:, p, :], PS[:, 0, D:2 * D], ACT.Copy).then_inc(x3T_ready, 1)

        def copy_probs(n):
            act.wait_ge(tp_done, n + 1)
            r = HK - 9 * P
            for out, bank in ((pcT[:, 0:4, :], PS[:, 4, :]), (pcT[:, 4:8, :], PS[:, 5, :]), (pcT[:, 8, :], PS[:, 6, 0:P]),
                              (pcT[0:r, 9, :], PS[0:r, 6, P:2 * P])):
                act.activation(out.rearrange("p c n -> p (c n)") if len(out.shape) == 3 else out, bank,
                               ACT.Copy).then_inc(tp_act, 1)

        def body(b, n, p):
            copy_probs(n)
            if exists(n + 1):
                numerators(n + 1, 1 - p, 0)
                numerators(n + 1, 1 - p, 1)
            if exists(n + 2):
                copy_turned(n + 2, p)
            if exists(n - 1):
                copy_x3T(n - 1, 1 - p)

        copy_turned(0, 0)
        copy_turned(1, 1)
        for part in range(2):
            numerators(0, 0, part)
        pairs(act, body)
        copy_x3T(NT - 1, 1)

    def pool_cross(pool):
        def root(n, i, p, row_var, var, done):
            wait_apart(pool, row_var, n + 1, waited_pool)
            pool.tensor_scalar(rs1[:, i, p:p + 1], mv1[:, i, p, 1:2], LN_EPS, None, ALU.add).then_inc(var, 1)
            pool.wait_ge(var, n + 1)
            pool.tensor_tensor(rs1[:, i, p:p + 1], rs1[:, i, p:p + 1], minus_half[:, 0:1], ALU.pow).then_inc(done, 1)

        def add_biases(n, p):
            pool.wait_ge(c_z, n + 1)
            if exists(n - 2):
                pool.wait_ge(res_ready, n - 1)
            pool.tensor_tensor(zbo[:, p, :], zc[:, p, :], bob[:], ALU.add).then_inc(c_zb, 1)
            pool.tensor_tensor(X[:, n, :], X[:, n, :], lnbb[:], ALU.add).then_inc(x_beta, 1)

        def x3_root(n):
            wait_apart(pool, x3_var, 2 * n + 6, waited_pool)
            once = rs[:, 0, ds(n, 1)]
            pool.tensor_tensor(once, once, minus_half[:, 0:1], ALU.pow).then_inc(x3_once, 1)

        def divide_first(n, p):
            h0, h1 = PARTS[0]
            pr = pc[:, p, h0 * C:h1 * C].rearrange("p (h c) -> p h c", c=C)
            pool.wait_ge(c_sum, 4 * n + 2)
            pool.tensor_tensor(pr, pr, by_head(sum1, p, h0, h1), ALU.mult).then_inc(pnorm_ready, 1)

        def keep_x3(n, p):
            wait_apart(pool, x3_ready, n + 1, waited_pool)
            pool.tensor_copy(X[:, n, :], x3[:, p, :]).then_inc(x3_copied, 1)

        def body(b, n, p):
            if exists(n + 2):
                root(n + 2, 0, p, c_stats, c_var, c_rstd)
            if exists(n - 1):
                keep_x3(n - 1, 1 - p)
            if exists(n + 1):
                divide_first(n + 1, 1 - p)
            root(n, 1, p, r_stats, r_var, r_rstd)
            if exists(n + 2):
                add_biases(n + 2, p)
            if exists(n - 2):
                x3_root(n - 2)

        pool.wait_ge(cross_in, 16 * CROSS_LOADS)
        pool.wait_ge(tanh_ready, 1)
        pool.tensor_scalar(lngb[:], lngb[:], tg[:, 1:2], None, ALU.mult).then_inc(lnb_scaled, 1)
        pool.tensor_scalar(lnbb[:], lnbb[:], tg[:, 1:2], None, ALU.mult).then_inc(lnb_scaled, 1)
        pool.wait_ge(lnb_scaled, 2)
        for n in range(2):
            root(n, 0, n, c_stats, c_var, c_rstd)
            add_biases(n, n)
        divide_first(0, 0)
        pairs(pool, body)
        keep_x3(NT - 1, 1)
        for n in (NT - 2, NT - 1):
            x3_root(n)

    CROSS_LOADS = 5

    def sp_cross(sp):
        sp.wait_ge(fold_read, FOLD_ALL)
        sp.wait_ge(vwo_read, H1 * B)
        sp.dma_start(bob[:], t["L1_xattn_bo"].partition_broadcast(P)).then_inc(cross_in, 16)
        sp.dma_start(lngb[:], t["L1_xattn_ln_gamma"].partition_broadcast(P)).then_inc(cross_in, 16)
        sp.dma_start(lnbb[:], t["L1_xattn_ln_beta"].partition_broadcast(P)).then_inc(cross_in, 16)
        sp.dma_start(wr[:], t["L1_ffn_Wr"].rearrange("(k p) n -> p k n", p=P)).then_inc(cross_in, 16)
        sp.dma_start(brb[:], t["L1_ffn_br"].partition_broadcast(P)).then_inc(cross_in, 16)

    def pool_consts(pool):
        pool.memset(fill[:], NO_TOKEN).then_inc(const_set, 1)
        pool.memset(upper[:], 1.0).then_inc(const_set, 1)
        pool.memset(onesq[:], 1.0).then_inc(const_set, 1)
        pool.iota(iotas[:, 0, 0:E], pattern=[[1, E]], base=-E, channel_multiplier=0,
                  allow_small_or_imprecise_dtypes=True).then_inc(const_set, 1)
        pool.iota(iotas[:, 1, 0:SLOTS], pattern=[[1, SLOTS]], base=0, channel_multiplier=0,
                  allow_small_or_imprecise_dtypes=True).then_inc(const_set, 1)
        pool.iota(iotas[:, 2, 0:NT], pattern=[[P, NT]], base=0, channel_multiplier=1,
                  allow_small_or_imprecise_dtypes=True).then_inc(const_set, 1)
        pool.wait_ge(const_set, 6)
        pool.affine_select(out=upper[:], in_=upper[:], compare_op=ALU.is_gt, fill=0.0, base=0,
                           pattern=[[1, P]], channel_multiplier=-1).then_inc(const_set, 1)

    def pool_fill(pool):
        rows = t["sorted"].rearrange("(n p) r -> p n r", p=P)
        for p, (n0, n1) in enumerate(((0, SLOTS // 2), (SLOTS // 2, SLOTS))):
            pool.dma_start(rows[:, n0:n1, :], fill[:].unsqueeze(1).to_broadcast([P, n1 - n0, ROW]))                 .then_inc(out_rows[p], 16)

    flat = lambda v: v.rearrange("p t e -> p (t e)")

    def pe_route(pe):
        pe.wait_ge(x3T_ready, NT)
        pe.wait_ge(sc_read, 2 * NT)
        pe.wait_ge(const_set, 7)
        for k in range(KC):
            last = pe.matmul(PS[:, 2, 0:E], onesq[:], wr[:, k, :], start=k == 0, stop=k == KC - 1)
        last.then_inc(wr_summed, 1)
        pe.wait_ge(oh_ready, 1)
        pe.matmul(PS[:, 0, 0:NT * E], upper[:], flat(RT[:, 1]), start=True, stop=True)
        pe.matmul(PS[:, 1, 0:NT * E], onesq[:], flat(RT[:, 1]), start=True, stop=True).then_inc(rank_done, 1)

    def act_route(act):
        act.wait_ge(gexp_in, 1)
        act.activation(RT[:, 0], RT[:, 0], ACT.Exp).then_inc(gexp_ready, 1)

    def dve_route(dve):
        own = Count(dve, route_own)
        onehot, rank, total, ca, cb, slots_of = RT[:, 1], RT[:, 2], RT[:, 3], RT[:, 4], RT[:, 5], RT[:, 6]
        small = lambda k: RT[:, 7 + k // NT, k % NT, :]
        bc_t = lambda v: v.unsqueeze(1).to_broadcast([P, NT, E])
        bc_e = lambda v: v.unsqueeze(2).to_broadcast([P, NT, E])
        dve.wait_ge(const_set, 7)
        dve.wait_ge(lg_ready, NT + 1)
        once, twice = rs[:, 0, 0:NT], rs[:, 1, 0:NT]
        dve.wait_ge(x3_var, 2 * NT + 4)
        dve.wait_ge(x3_once, NT)
        dve.wait_ge(wr_summed, 1)
        own.add(dve.tensor_copy(small(0), PS[:, 2, 0:E]))
        normalized_twice(dve, own, meanvar[:, 0:NT, 1], once, twice)
        own.add(dve.tensor_tensor(RT[:, 0], bc_t(small(0)), bc_e(meanvar[:, 0:NT, 0]), ALU.mult))
        own.wait()
        own.add(dve.tensor_tensor(LG[:], LG[:], RT[:, 0], ALU.subtract))
        own.add(dve.tensor_copy(XR[:, :, MEAN], meanvar[:, 0:NT, 0]))
        own.add(dve.tensor_copy(XR[:, :, TOKEN], iotas[:, 2, 0:NT]))
        own.wait()
        own.add(dve.tensor_tensor(LG[:], LG[:], bc_e(once), ALU.mult))
        own.wait()
        own.add(dve.tensor_tensor(LG[:], LG[:], bc_t(brb[:]), ALU.add))
        own.wait()
        own.add(dve.tensor_reduce(rtn[:, 3, :], LG[:], AX.X, ALU.max))
        own.wait()
        dve.tensor_tensor(RT[:, 0], LG[:], bc_e(rtn[:, 3, :]), ALU.subtract).then_inc(gexp_in, 1)
        own.add(dve.tensor_tensor(RT[:, 2], LG[:], bc_e(rtn[:, 3, :]), ALU.is_equal))
        own.wait()
        own.add(dve.tensor_tensor(RT[:, 2], RT[:, 2], bc_t(iotas[:, 0, 0:E]), ALU.mult))
        own.wait()
        own.add(dve.tensor_reduce(rtn[:, 0, :], RT[:, 2], AX.X, ALU.min))
        own.wait()
        dve.tensor_tensor(onehot, bc_t(iotas[:, 0, 0:E]), bc_e(rtn[:, 0, :]), ALU.is_equal).then_inc(oh_ready, 1)
        dve.wait_ge(gexp_ready, 1)
        own.add(dve.tensor_reduce(rtn[:, 1, :], RT[:, 0], AX.X, ALU.add))
        own.wait()
        own.add(dve.reciprocal(rtn[:, 1, :], rtn[:, 1, :]))
        own.wait()
        own.add(dve.tensor_scalar(XR[:, :, GATE], rtn[:, 1, :], tg[:, 3:4], None, ALU.mult))
        dve.wait_ge(root_out, 3)
        own.add(dve.tensor_tensor(XR[:, :, ROOT], twice, once, ALU.mult))
        dve.wait_ge(rank_done, 1)
        own.add(dve.tensor_copy(flat(rank), PS[:, 0, 0:NT * E]))
        own.add(dve.tensor_copy(flat(total), PS[:, 1, 0:NT * E]))
        own.wait()
        src, dst, step = total, ca, 1
        while step < NT:
            own.add(dve.tensor_copy(dst[:, 0:step, :], src[:, 0:step, :]))
            own.add(dve.tensor_tensor(dst[:, step:, :], src[:, step:, :], src[:, 0:NT - step, :], ALU.add))
            own.wait()
            src, dst, step = dst, (cb if dst is ca else ca), 2 * step
        counts = src[:, NT - 1, :]
        own.add(dve.tensor_scalar(small(0), counts, float(P - 1), None, ALU.add))
        own.wait()
        own.add(dve.tensor_copy(rti[:, 0:E], small(0)))
        own.wait()
        own.add(dve.tensor_scalar(rti[:, 0:E], rti[:, 0:E], P.bit_length() - 1, None, ALU.arith_shift_right))
        own.wait()
        own.add(dve.tensor_copy(small(1), rti[:, 0:E]))
        own.wait()
        tiles, at, step = small(1), 2, 1
        total_tiles = tiles
        while step < E:
            nxt = small(at)
            own.add(dve.tensor_copy(nxt[:, 0:step], total_tiles[:, 0:step]))
            own.add(dve.tensor_tensor(nxt[:, step:], total_tiles[:, step:], total_tiles[:, 0:E - step], ALU.add))
            own.wait()
            total_tiles, at, step = nxt, at + 1, 2 * step
        first_row = small(at)
        own.add(dve.tensor_tensor(first_row, total_tiles, tiles, ALU.subtract))
        own.add(dve.tensor_tensor(slots_of, src, total, ALU.subtract))
        own.wait()
        own.add(dve.tensor_scalar(first_row, first_row, float(P), None, ALU.mult))
        own.add(dve.tensor_tensor(slots_of, slots_of, rank, ALU.add))
        own.wait()
        own.add(dve.tensor_tensor(slots_of, slots_of, bc_t(first_row), ALU.add))
        own.wait()
        own.add(dve.tensor_tensor(slots_of, slots_of, onehot, ALU.mult))
        own.wait()
        own.add(dve.tensor_reduce(rtn[:, 2, :], slots_of, AX.X, ALU.add))
        own.wait()
        own.add(dve.tensor_copy(slot[:], rtn[:, 2, :]))
        own.wait()
        dve.engine_nop().then_inc(slot_ready, 1)
        ends = RT[:, 0:2].rearrange("p a t e -> p (a t) e")[:, 0:SLOTS, :]
        own.add(dve.tensor_tensor(ends, total_tiles.unsqueeze(1).to_broadcast([P, SLOTS, E]),
                                  iotas[:, 1, 0:SLOTS].unsqueeze(2).to_broadcast([P, SLOTS, E]), ALU.is_le))
        own.wait()
        own.add(dve.tensor_reduce(top[:, 0:4, :].rearrange("p a b -> p (a b)")[:, 0:SLOTS], ends, AX.X, ALU.add))
        own.wait()
        dve.tensor_scalar(expert_of[:], top[:, 0:4, :].rearrange("p a b -> p (a b)")[:, 0:SLOTS], float(E - 1), None,
                          ALU.min).then_inc(expert_ready, 1)

    def pool_route(pool):
        pool.wait_ge(root_in, 3)
        pool.tensor_tensor(rs[:, 1, 0:NT], rs[:, 1, 0:NT], minus_half[:, 0:NT], ALU.pow).then_inc(root_out, 1)
        pool.wait_ge(slot_ready, 1)
        for p in range(2):
            pool.wait_ge(out_rows[p], 16)
        for n in range(NT):
            pool.indirect_dma_start(t["sorted"], bass.IndirectOffsetOnAxis(ap=slot[:, n:n + 1], axis=0),
                                    XR[:, n, :], None).then_inc(scattered, 16)

    def sp_experts_loads(sp):
        sp.wait_ge(lif_done, 2 * NG + 2)
        for e in range(E):
            sp.dma_start(w1[:, e, :, :], t["L1_ffn_W1"][e].rearrange("(k p) f -> p k f", p=P)).then_inc(w1_in, 16)
        sp.wait_ge(pvc_done, NT)
        for e in range(E):
            sp.dma_start(w2[:, e, :, :], t["L1_ffn_W2"][e].rearrange("(c p) d -> p c d", p=P)).then_inc(w2_in, 16)
        sp.wait_ge(oh_ready, 1)
        sp.dma_start(b2[:], t["L1_ffn_b2"].rearrange("e d -> (e d)").partition_broadcast(P)).then_inc(b2_in, 16)

    def slot_tiles(eng, body):
        rounds = (SLOTS - 2) // 4
        with eng.Fori(0, rounds) as i:
            for u in range(4):
                body(4 * i + u, u, True, True)
        for n in range(4 * rounds, SLOTS):
            body(n, n % 4, n + 1 < SLOTS, n + 2 < SLOTS)

    def sp_experts(sp):
        def load(n, u, nxt, after):
            sp.wait_ge(oe_ready, n + 1)
            sp.dma_start(xe[:, u, :], t["sorted"][ds(n * P, P), :]).then_inc(xe_in[u], 16)
        sp.wait_ge(scattered, 16 * NT)
        slot_tiles(sp, load)

    of_buffer = lambda n, u: 4 * n + (16 - 4 * u)
    of_parity = lambda n, p: 8 * n + (16 - 8 * p)

    def dve_experts(dve):
        def norm(n, u):
            p = u % 2
            dve.wait_ge(xe_in[u], of_buffer(n, u))
            dve.tensor_scalar(ze[:, p, :], xe[:, u, 0:D], xe[:, u, MEAN:MEAN + 1], xe[:, u, ROOT:ROOT + 1],
                              ALU.subtract, ALU.mult).then_inc(e_z, 1)

        def hidden(n, p):
            dve.wait_ge(g1_done, n + 1)
            dve.tensor_copy(he[:, 512:F], PS[:, 2 + 5 * p, :]).then_inc(he_dve, 1)

        def activate(n, p):
            e = dve.value_load(expert_of[0:1, ds(n, 1)], min_val=0, max_val=E - 1)
            dve.wait_ge(heT_done, n + 1)
            for c in range(4, FC):
                last = dve.tensor_scalar(heT[:, c, :], PS[:, 4, (c - 4) * P:(c - 3) * P], b1f[:, ds(e * FC + c, 1)], 0.0,
                                         ALU.add, ALU.max)
            last.then_inc(heT_dve, 1)

        def finish(n, u):
            p = u % 2
            dve.wait_ge(out_rows[p], of_parity(n, p))
            dve.tensor_copy(token[:, p:p + 1], xe[:, u, TOKEN:TOKEN + 1]).then_inc(e_token, 1)
            e = dve.value_load(expert_of[0:1, ds(n, 1)], min_val=0, max_val=E - 1)
            dve.wait_ge(g2_done, n + 1)
            dve.tensor_tensor(oe[:, p, :], PS[:, 5, 0:D], b2[:, ds(e * D, D)], ALU.add).then_inc(e_biased, 1)
            dve.wait_ge(e_biased, n + 1)
            dve.scalar_tensor_tensor(oe[:, p, :], oe[:, p, :], xe[:, u, GATE:GATE + 1], xe[:, u, 0:D],
                                     ALU.mult, ALU.add).then_inc(oe_ready, 1)

        def body(n, u, nxt, after):
            if after:
                norm(n + 2, (u + 2) % 4)
            activate(n, u % 2)
            if nxt:
                hidden(n + 1, 1 - u % 2)
            finish(n, u)
        dve.wait_ge(expert_ready, 1)
        dve.wait_ge(moe_in, 48)
        dve.wait_ge(b2_in, 16)
        norm(0, 0)
        norm(1, 1)
        hidden(0, 0)
        slot_tiles(dve, body)

    b1f = b1[:].rearrange("p e c -> p (e c)")

    def act_experts(act):
        def affine(n, p):
            act.wait_ge(e_zT, n + 1)
            for k in range(KC):
                last = act.activation(xeT[:, p, k, :], PS[:, 0, k * P:k * P + P], ACT.Identity,
                                      bias=leb[:, k:k + 1], scale=leg[:, k:k + 1])
            last.then_inc(e_zT_ready, 1)

        def hidden(n, p):
            act.wait_ge(g1_done, n + 1)
            act.activation(he[:, 0:512], PS[:, 1 + 5 * p, :], ACT.Copy).then_inc(he_act, 1)

        def activate(n, p):
            e = act.value_load(expert_of[0:1, ds(n, 1)], min_val=0, max_val=E - 1)
            act.wait_ge(heT_done, n + 1)
            for c in range(4):
                last = act.activation(heT[:, c, :], PS[:, 3, c * P:c * P + P], ACT.Relu, bias=b1f[:, ds(e * FC + c, 1)])
            last.then_inc(heT_act, 1)

        def body(n, u, nxt, after):
            p = u % 2
            activate(n, p)
            if nxt:
                hidden(n + 1, 1 - p)
            if after:
                affine(n + 2, p)
        act.wait_ge(expert_ready, 1)
        act.wait_ge(moe_in, 48)
        affine(0, 0)
        hidden(0, 0)
        affine(1, 1)
        slot_tiles(act, body)

    def pe_experts(pe):
        def turn(n, p):
            pe.wait_ge(e_z, n + 1)
            for k in range(KC):
                last = pe.transpose(PS[:, 0, k * P:k * P + P], ze[:, p, k * P:k * P + P], ident[:])
            last.then_inc(e_zT, 1)

        def up(n, p):
            e = pe.value_load(expert_of[0:1, ds(n, 1)], min_val=0, max_val=E - 1)
            pe.wait_ge(e_zT_ready, n + 1)
            w = w1[:].rearrange("p e k f -> p (e k f)")
            for half in range(2):
                for k in range(KC):
                    last = pe.matmul(PS[:, 1 + half + 5 * p, :], xeT[:, p, k, :], w[:, ds(e * (KC * F) + k * F + half * 512, 512)],
                                     start=k == 0, stop=k == KC - 1)
            last.then_inc(g1_done, 1)

        def turn_hidden(n, p):
            pe.wait_ge(he_act, n + 1)
            pe.wait_ge(he_dve, n + 1)
            for c in range(FC):
                last = pe.transpose(PS[:, 3 + c // 4, c % 4 * P:c % 4 * P + P], he[:, c * P:c * P + P], ident[:])
            last.then_inc(heT_done, 1)

        def down(n, p):
            e = pe.value_load(expert_of[0:1, ds(n, 1)], min_val=0, max_val=E - 1)
            pe.wait_ge(oe_ready, n + 4)
            pe.wait_ge(heT_act, n + 1)
            pe.wait_ge(heT_dve, n + 1)
            w = w2[:].rearrange("p e c d -> p (e c d)")
            for c in range(FC):
                last = pe.matmul(PS[:, 5, 0:D], heT[:, c, :], w[:, ds(e * (FC * D) + c * D, D)], start=c == 0,
                                 stop=c == FC - 1)
            last.then_inc(g2_done, 1)

        def body(n, u, nxt, after):
            p = u % 2
            turn_hidden(n, p)
            if nxt:
                up(n + 1, 1 - p)
            if after:
                turn(n + 2, p)
            down(n, p)
        pe.wait_ge(expert_ready, 1)
        pe.wait_ge(w1_in, 16 * E)
        turn(0, 0)
        up(0, 0)
        turn(1, 1)
        pe.wait_ge(w2_in, 16 * E)
        slot_tiles(pe, body)

    def pool_experts(pool):
        def send(n, p):
            pool.wait_ge(oe_ready, n + 5)
            wait_apart(pool, e_token, n + 1, waited_pool)
            pool.indirect_dma_start(t["out"].rearrange("b s d -> (b s) d"),
                                    bass.IndirectOffsetOnAxis(ap=token[:, p:p + 1], axis=0), oe[:, p, :], None,
                                    bounds_check=B * S - 1, oob_is_err=False).then_inc(out_rows[p], 16)

        def body(n, u, nxt, after):
            send(n, u % 2)
        slot_tiles(pool, body)
        for p in range(2):
            pool.wait_ge(out_rows[p], 16 + 16 * ((SLOTS + 1 - p) // 2))

    block = ctx.enter_context(nc.Block())

    @block.sync
    def _(sp):
        xv = t["x"].rearrange("b (t p) d -> p (b t) d", p=P)
        load_x = lambda g: sp.dma_start(X[:, GT * g:GT * g + GT, :], xv[:, GT * g:GT * g + GT, :]).then_inc(x_in[g], 16)
        for g in range(NG):
            load_x(g)
        sp.wait_ge(zero_set, 1)
        sp.dma_start(ctxn[0:C, :, :], t["ctx_1024"].rearrange("b c d -> c b d")).then_inc(ctx_in, 16)
        sp.dma_start(wqkv[:, :, 0:D], t["L0_xattn_W_q"].rearrange("(k p) n -> p k n", p=P)).then_inc(wts_in, 16)
        sp.dma_start(wqkv[:, :, D:3 * D], t["L0_xattn_W_kv"].rearrange("(k p) n -> p k n", p=P)).then_inc(wts_in, 16)
        for lo in (0, E0):
            sp.dma_start(wout[lo:lo + E0], t["L0_xattn_W_out"].rearrange("(h e) n -> e h n", e=E0)).then_inc(wts_in, 16)
        sp.wait_ge(vec_in, 16 * VECS)
        for w, name in ((wk1, "L1_xattn_Wk"), (wv1, "L1_xattn_Wv"), (wq1, "L1_xattn_Wq")):
            sp.dma_start(w[:], t[name].rearrange("(k p) n -> p k n", p=P)).then_inc(fold_in, 16)
        sp.dma_start(wo1[:], t["L1_xattn_Wo"].rearrange("(c p) n -> p c n", p=P)).then_inc(fold_in, 16)
        sp_fold(sp)
        sp_cross(sp)
        sp_experts_loads(sp)
        sp_experts(sp)

    @block.gpsimd
    def _(pool):
        pool.memset(ctxn[:], 0.0).then_inc(zero_set, 1)
        pool.memset(ident[:], 0.0).then_inc(ident_set, 1)
        pool.memset(minus_half[:], -0.5).then_inc(half_set, 1)
        pool.wait_ge(ident_set, 1)
        pool.affine_select(out=ident[:], in_=ident[:], compare_op=ALU.not_equal, fill=1.0, base=0,
                           pattern=[[-1, P]], channel_multiplier=1).then_inc(ident_set, 1)
        pool_norm(pool)
        pool_consts(pool)
        pool.wait_ge(wts_in, 64)
        pool.wait_ge(tanh_ready, 1)
        pool.tensor_scalar(wout[:], wout[:], tg[:, 0:1], None, ALU.mult).then_inc(wout_scaled, 1)
        pool.tensor_scalar(boutb[:], boutb[:], tg[:, 0:1], None, ALU.mult).then_inc(wout_scaled, 1)
        pool.tensor_scalar(tg5[:], tg[:, 2:3], 0.2, None, ALU.mult).then_inc(tg_ready, 1)
        pool.wait_ge(wout_scaled, 2)
        with pool.Fori(0, B) as b:
            pool_project(pool, b)
        pool.wait_ge(proj_added, GT * MP * B)
        pool.memset(keysT[:].rearrange("p c b a n -> p (c b a n)"), 0.0).then_inc(zeroed, 1)
        pool_fill(pool)
        pool_ffn(pool)
        pool_cross(pool)
        pool_route(pool)
        pool_experts(pool)

    @block.scalar
    def _(act):
        def column(dst, name, k, done=vec_in):
            act.dma_start(dst, t[name].rearrange("(k p) -> p k", k=k),
                          allow_slow_non_contiguous=True).then_inc(done, 16)
        act.dma_start(gates[:, 0:2], t["g_xattn"].partition_broadcast(P)).then_inc(vec_in, 16)
        act.dma_start(gates[:, 2:4], t["g_ffn"].partition_broadcast(P)).then_inc(vec_in, 16)
        act.dma_start(boutb[:], t["L0_xattn_b_out"].partition_broadcast(P)).then_inc(vec_in, 16)
        column(lnlg[:], "L0_xattn_ln_l_g", KC)
        column(lnlb[:], "L0_xattn_ln_l_b", KC)
        column(lnxg[:], "L0_xattn_ln_x_g", KC)
        column(lnxb[:], "L0_xattn_ln_x_b", KC)
        for lo in (0, E0):
            column(qgam[lo:lo + E0, :], "L0_xattn_q_gamma", 1)
            column(kgam[lo:lo + E0, :], "L0_xattn_k_gamma", 1)
        act.dma_start(masku[:], t["mask_BxS2_bk0"].rearrange("(a b) c -> a b c", a=1)).then_inc(vec_in, 16)
        for done, dst, name, k in ((l1_in, bq1[:], "L1_xattn_bq", FC), (l1_in, bk1[:], "L1_xattn_bk", FC), (l1_in, bv1[:], "L1_xattn_bv", FC),
                                   (moe_in, leg[:], "L1_ffn_ln_g", KC), (moe_in, leb[:], "L1_ffn_ln_b", KC)):
            column(dst, name, k, done)
        act.dma_start(b1[:], t["L1_ffn_b1"].rearrange("e (c p) -> p e c", p=P),
                      allow_slow_non_contiguous=True).then_inc(moe_in, 16)
        act.wait_ge(vec_in, 16 * VECS)
        act.activation(tg[:], gates[:], ACT.Tanh).then_inc(tanh_ready, 1)
        act.wait_ge(gam_scaled, 1)
        with act.Fori(0, B) as b:
            act_project(act, b)
            act_attend(act, b)
        act_fold(act)
        act_ffn(act)
        act_cross(act)
        act_route(act)
        act_experts(act)

    @block.tensor
    def _(pe):
        pe.wait_ge(ident_set, 2)
        pe.wait_ge(wts_in, 64)
        pe.wait_ge(mask_set, 2)
        pe.wait_ge(ones_set, 3)
        with pe.Fori(0, B) as b:
            pe_project(pe, b)
            pe_attend(pe, b)
        pe_fold(pe)
        pe_ffn(pe)
        pe_cross(pe)
        pe_route(pe)
        pe_experts(pe)

    @block.vector
    def _(dve):
        dve_norm(dve)
        dve.wait_ge(vec_in, 16 * VECS)
        dve.tensor_scalar(qgam[:], qgam[:], E0 ** -0.5, None, ALU.mult).then_inc(gam_scaled, 1)
        dve.memset(maskr[:].bitcast(F32), 0.0).then_inc(mask_set, 1)
        dve.wait_ge(mask_set, 1)
        dve.tensor_scalar(maskr[:, :, 0:C], masku[:], 1.0, MASKED, ALU.subtract, ALU.mult).then_inc(mask_set, 1)
        dve.memset(ones33[:].bitcast(F32), 0.0).then_inc(ones_set, 1)
        dve.wait_ge(ones_set, 1)
        dve.memset(ones33[0:1, :].bitcast(F32), 1.0).then_inc(ones_set, 1)
        dve.memset(ones33[32:33, :].bitcast(F32), 1.0).then_inc(ones_set, 1)
        dve.memset(rsg[:, 0:1], 0.0).then_inc(lif_done, 2)
        dve.memset(rsg[:, 1:2], 0.0).then_inc(y_done, 1)
        dve.memset(rsg[:, 2:3], 0.0).then_inc(oe_ready, 4)
        dve.memset(nmax[:, 0, 0:1], 0.0).then_inc(pv_done, PB)
        dve.memset(nmax[:, 0, 1:2], 0.0).then_inc(lg_ready, 1)
        dve.memset(nmax[:, 0, 2:3], 0.0).then_inc(x3_stats, 1)
        dve.memset(nmax[:, 0, 3:4], 0.0).then_inc(x3_var, 4)
        with dve.Fori(0, B) as b:
            dve_project(dve, b)
            dve_attend(dve, b)
        dve_fold(dve)
        dve.wait_ge(tg_ready, 1)
        dve_ffn(dve)
        dve_cross(dve)
        dve_route(dve)
        dve_experts(dve)
    ctx.close()


def build(nc, shapes):
    t = {}
    for name, (shape, dt) in shapes.items():
        t[name] = nc.dram_tensor(f"in_{name}", list(shape), dt, kind="ExternalInput").ap()
    t["out"] = nc.dram_tensor("out", [B, S, D], F32, kind="ExternalOutput").ap()
    t["vw_rows"] = nc.dram_tensor("vw_rows", [B, HK, D], F32).ap()
    t["sorted"] = nc.dram_tensor("sorted", [SLOTS * P, ROW], F32).ap()
    layers_kernel(nc, t)


def kernel(**inputs):
    import concourse.bacc as bacc
    from concourse.bass_utils import run_bass_kernel_spmd

    nc = bacc.Bacc("TRN2", target_bir_lowering=False, num_devices=1)
    arrays, shapes = {}, {}
    for name, a in inputs.items():
        a = np.ascontiguousarray(a)
        arrays[f"in_{name}"] = a
        shapes[name] = (a.shape, mybir.dt.from_np(a.dtype))
    build(nc, shapes)
    r = run_bass_kernel_spmd(nc, [arrays], core_ids=[0])
    return r.results[0]["out"]
```
